# Optimizing a Trainium2 kernel written in Bass

```python
import numpy as np
import jax
import jax.numpy as jnp

def _softmax(x, axis=-1):
    return jax.nn.softmax(x, axis=axis)

def _gelu(x):
    return jax.nn.gelu(x, approximate=True)

def _silu(x):
    return jax.nn.silu(x)

def _sigmoid(x):
    return jax.nn.sigmoid(x)

def _layernorm(x, axis=-1, eps=1e-05):
    m = jnp.mean(x, axis=axis, keepdims=True)
    v = jnp.var(x, axis=axis, keepdims=True)
    return (x - m) / jnp.sqrt(v + eps)

def _scatter_add(tgt, idx, src, axis=0):
    return tgt.at[idx].add(src)

def _segment_sum(src, seg, n):
    return jax.ops.segment_sum(src, seg, n)
kernel_name = 'mk_macaron_d1_jaxref_r8_10a83b'

def setup_inputs(seed: int=0):
    np.random.seed(seed)
    _w = jnp.asarray

    def _L0_attn_setup():
        import jax, jax.numpy as jnp
        import numpy as np
        D_MODEL = 128
        N_HEADS = 16
        HEAD_DIM = D_MODEL // N_HEADS
        MAX_LEN = 256
        BATCH = 2
        SEQ = 256
        key = jax.random.key(seed)
        ks = jax.random.split(key, 10)
        s = 1.0 / np.sqrt(D_MODEL)
        inp = {'x': jax.random.normal(ks[0], (BATCH, SEQ, D_MODEL), dtype=jnp.float32), 'Wq': jax.random.uniform(ks[1], (D_MODEL, D_MODEL), jnp.float32, -s, s), 'bq': jax.random.uniform(ks[2], (D_MODEL,), jnp.float32, -s, s), 'Wk': jax.random.uniform(ks[3], (D_MODEL, D_MODEL), jnp.float32, -s, s), 'bk': jax.random.uniform(ks[4], (D_MODEL,), jnp.float32, -s, s), 'Wv': jax.random.uniform(ks[5], (D_MODEL, D_MODEL), jnp.float32, -s, s), 'bv': jax.random.uniform(ks[6], (D_MODEL,), jnp.float32, -s, s), 'Wo': jax.random.uniform(ks[7], (D_MODEL, D_MODEL), jnp.float32, -s, s), 'bo': jax.random.uniform(ks[8], (D_MODEL,), jnp.float32, -s, s), 'rel_emb': jax.random.normal(ks[9], (MAX_LEN * 2 - 1, HEAD_DIM), dtype=jnp.float32)}
        return inp
    _L0_attn_in = _L0_attn_setup()

    def _L0_ffn_setup():
        import jax, jax.numpy as jnp
        import numpy as np
        LN_EPS = 1e-05

        def _swiglu(h, w_gate_up, w_down):
            gu = h @ w_gate_up.T
            gate, up = jnp.split(gu, 2, axis=-1)
            return jax.nn.silu(gate) * up @ w_down.T
        key = jax.random.key(seed)
        ks = jax.random.split(key, 6)
        d_model, d_ff, E = (128, 512, 8)
        shared_d_ff = d_ff // 4
        routed_d_ff = d_ff - shared_d_ff
        B, S = (4, 256)
        x = jax.random.normal(ks[0], (B, S, d_model), dtype=jnp.float32)
        ln_gamma = jnp.ones((d_model,), jnp.float32)
        ln_beta = jnp.zeros((d_model,), jnp.float32)
        router_w = jax.random.normal(ks[1], (E, d_model), jnp.float32) * 0.02
        gate_up_w = jax.random.normal(ks[2], (E, 2 * routed_d_ff, d_model), jnp.float32) * (1.0 / np.sqrt(d_model))
        down_w = jax.random.normal(ks[3], (E, d_model, routed_d_ff), jnp.float32) * (1.0 / np.sqrt(routed_d_ff))
        shared_gate_up_w = jax.random.normal(ks[4], (2 * shared_d_ff, d_model), jnp.float32) * (1.0 / np.sqrt(d_model))
        shared_down_w = jax.random.normal(ks[5], (d_model, shared_d_ff), jnp.float32) * (1.0 / np.sqrt(shared_d_ff))
        return dict(x=x, ln_gamma=ln_gamma, ln_beta=ln_beta, router_w=router_w, gate_up_w=gate_up_w, down_w=down_w, shared_gate_up_w=shared_gate_up_w, shared_down_w=shared_down_w)
    _L0_ffn_in = _L0_ffn_setup()
    _d = {'L0_attn_x': _L0_attn_in['x'], 'L0_attn_Wq': _L0_attn_in['Wq'], 'L0_attn_bq': _L0_attn_in['bq'], 'L0_attn_Wk': _L0_attn_in['Wk'], 'L0_attn_bk': _L0_attn_in['bk'], 'L0_attn_Wv': _L0_attn_in['Wv'], 'L0_attn_bv': _L0_attn_in['bv'], 'L0_attn_Wo': _L0_attn_in['Wo'], 'L0_attn_bo': _L0_attn_in['bo'], 'L0_attn_rel_emb': _L0_attn_in['rel_emb'], 'L0_ffn_ln_gamma': _L0_ffn_in['ln_gamma'], 'L0_ffn_ln_beta': _L0_ffn_in['ln_beta'], 'L0_ffn_router_w': _L0_ffn_in['router_w'], 'L0_ffn_gate_up_w': _L0_ffn_in['gate_up_w'], 'L0_ffn_down_w': _L0_ffn_in['down_w'], 'L0_ffn_shared_gate_up_w': _L0_ffn_in['shared_gate_up_w'], 'L0_ffn_shared_down_w': _L0_ffn_in['shared_down_w']}
    _x0 = _d['L0_attn_x']
    _d['L0_attn_x'] = jax.random.normal(jax.random.fold_in(jax.random.key(seed), 1), (16, 512, 128), dtype=_x0.dtype)
    del _x0
    return _d

def reference(L0_attn_x, L0_attn_Wq, L0_attn_bq, L0_attn_Wk, L0_attn_bk, L0_attn_Wv, L0_attn_bv, L0_attn_Wo, L0_attn_bo, L0_attn_rel_emb, L0_ffn_ln_gamma, L0_ffn_ln_beta, L0_ffn_router_w, L0_ffn_gate_up_w, L0_ffn_down_w, L0_ffn_shared_gate_up_w, L0_ffn_shared_down_w):

    def _L0_attn_ref(x, Wq, bq, Wk, bk, Wv, bv, Wo, bo, rel_emb):
        import jax, jax.numpy as jnp
        import numpy as np
        D_MODEL = 128
        N_HEADS = 16
        HEAD_DIM = D_MODEL // N_HEADS
        MAX_LEN = 256
        BATCH = 2
        SEQ = 256
        B, L, _ = x.shape

        def lin(x, W, b):
            return jnp.einsum('bld,ed->ble', x, W) + b

        def split_heads(t):
            return t.reshape(B, L, N_HEADS, HEAD_DIM).transpose(0, 2, 1, 3)
        q = split_heads(lin(x, Wq, bq))
        k = split_heads(lin(x, Wk, bk))
        v = split_heads(lin(x, Wv, bv))
        r = jnp.arange(L)
        idx = r[None, :] - r[:, None] + (MAX_LEN - 1)
        rel = rel_emb[idx]
        qk = jnp.einsum('bhld,bhrd->bhlr', q, k) / np.sqrt(HEAD_DIM)
        qk = qk + jnp.einsum('bhld,lrd->bhlr', q, rel)
        att = jax.nn.softmax(qk, axis=-1)
        out = jnp.einsum('bhlr,bhrd->bhld', att, v)
        out = out.transpose(0, 2, 1, 3).reshape(B, L, D_MODEL)
        return lin(out, Wo, bo)

    def _L0_ffn_ref(x, ln_gamma, ln_beta, router_w, gate_up_w, down_w, shared_gate_up_w, shared_down_w):
        import jax, jax.numpy as jnp
        import numpy as np
        LN_EPS = 1e-05

        def _swiglu(h, w_gate_up, w_down):
            gu = h @ w_gate_up.T
            gate, up = jnp.split(gu, 2, axis=-1)
            return jax.nn.silu(gate) * up @ w_down.T
        B, S, D = x.shape
        E = router_w.shape[0]
        top_k = 2
        xt = x.reshape(-1, D)
        mu = jnp.mean(xt, axis=-1, keepdims=True)
        var = jnp.mean(jnp.square(xt - mu), axis=-1, keepdims=True)
        normed = (xt - mu) * jax.lax.rsqrt(var + LN_EPS) * ln_gamma + ln_beta
        logits = normed.astype(jnp.float32) @ router_w.T
        probs = jax.nn.softmax(logits, axis=-1)
        top_v, top_i = jax.lax.top_k(probs, top_k)
        gates = jax.nn.softmax(top_v, axis=-1)
        comb = jnp.sum(jax.nn.one_hot(top_i, E, dtype=gates.dtype) * gates[..., None], axis=1)
        out = jnp.zeros_like(normed)
        for e in range(E):
            y = _swiglu(normed, gate_up_w[e], down_w[e])
            out = out + comb[:, e, None] * y
        out = out + _swiglu(normed, shared_gate_up_w, shared_down_w)
        return out.reshape(B, S, D)
    x = L0_attn_x
    x = x + 0.5 * _L0_ffn_ref(_layernorm(x, axis=-1), L0_ffn_ln_gamma, L0_ffn_ln_beta, L0_ffn_router_w, L0_ffn_gate_up_w, L0_ffn_down_w, L0_ffn_shared_gate_up_w, L0_ffn_shared_down_w)
    x = x + _L0_attn_ref(_layernorm(x, axis=-1), L0_attn_Wq, L0_attn_bq, L0_attn_Wk, L0_attn_bk, L0_attn_Wv, L0_attn_bv, L0_attn_Wo, L0_attn_bo, L0_attn_rel_emb)
    x = x + 0.5 * _L0_ffn_ref(_layernorm(x, axis=-1), L0_ffn_ln_gamma, L0_ffn_ln_beta, L0_ffn_router_w, L0_ffn_gate_up_w, L0_ffn_down_w, L0_ffn_shared_gate_up_w, L0_ffn_shared_down_w)
    return x

_drawn_inputs = setup_inputs


def setup_inputs(seed=0):
    import zlib

    import numpy as np

    out = dict(_drawn_inputs(seed))
    spreads = {'L0_ffn_ln_gamma': (1.0, 0.2), 'L0_ffn_ln_beta': (0.0, 0.1)}
    factors = {'L0_attn_bq': 3.994, 'L0_attn_bk': 8.0}
    for name, (base, spread) in spreads.items():
        noise = np.random.default_rng([zlib.crc32(name.encode()), seed]).standard_normal(out[name].shape)
        drawn = base * np.exp(spread * noise) if base else spread * noise
        out[name] = jnp.asarray(drawn.astype(out[name].dtype))
    for name, factor in factors.items():
        out[name] = (out[name] * factor).astype(out[name].dtype)
    return out
```

```python
from contextlib import ExitStack

import numpy as np

import concourse.bass as bass
from concourse import mybir

F32 = mybir.dt.float32
F32R = mybir.dt.float32r
ALU = mybir.AluOpType
ACT = mybir.ActivationFunctionType
AX = mybir.AxisListType.X

P = 128
D = 128
B, L = 16, 512
TOK = B * L
NT = TOK // P
JT = L // P
E, FF, SFF = 8, 384, 128
FC = FF // P
H, HD = 16, 8
MAXLEN = 256
LN_EPS = 1e-5
A8 = 8
NQ = L // A8
GT = 16
NG = NQ // GT
RELW = L + NQ - 1
KEYS32 = L // 32
REC = 2 * L + 2 * L + L


def slot_free(i, n, k):
    return i * n + max(k - 1, 0)


def snapped(eng, *values):
    for v in values:
        if not isinstance(v, int):
            eng.compute_val(v)
    return values


class Sems:

    def __init__(self, nc, ctx, prefix):
        self.nc, self.ctx, self.prefix, self.made = nc, ctx, prefix, {}

    def __call__(self, name):
        if name not in self.made:
            self.made[name] = self.ctx.enter_context(self.nc.semaphore(f"{self.prefix}_{name}"))
        return self.made[name]


def build(nc, T):
    with ExitStack() as top:
        def sb(ctx, name, shape, dt=F32):
            return ctx.enter_context(nc.sbuf_tensor(name, shape, dt))

        def ps(ctx, name, shape):
            return ctx.enter_context(nc.psum_tensor(name, shape, F32))

        def dram(name, shape):
            return nc.dram_tensor(name, shape, F32).ap()

        XR = sb(top, "residual", [P, NT, D])
        ident = sb(top, "ident", [P, P])
        mhalf = sb(top, "minus_half", [P, NT])
        gam = sb(top, "gamma_col", [P, 1])
        bet = sb(top, "beta_col", [P, 1])

        xn_t = dram("normed_T", [P, TOK])
        rec = dram("qkv_record", [B, P, REC])
        qd = dram("q_by_query", [B, 2, A8, P, NQ])
        rsd = dram("row_sums", [B * NG, P, GT])
        otd = dram("attn_out_T", [B, P, L])

        with nc.semaphore("load_in") as s_in, nc.semaphore("load_c") as s_c, nc.Block() as block:
            @block.sync
            def _(sp):
                xv = T["x"].rearrange("(n p) d -> p n d", p=P)
                for q in range(4):
                    sp.dma_start(XR[:, 16 * q:16 * q + 16, :], xv[:, 16 * q:16 * q + 16, :]).then_inc(s_in, 16)
                sp.wait_ge(s_in, 64)

            @block.scalar
            def _(act):
                act.dma_start(ident[:], T["ident"]).then_inc(s_c, 16)
                act.dma_start(gam[:], T["gamma"]).then_inc(s_c, 16)
                act.dma_start(bet[:], T["beta"]).then_inc(s_c, 16)
                act.wait_ge(s_c, 48)

            @block.vector
            def _(dve):
                nc.vector.memset(mhalf[:], -0.5)

        def ln_phase(tag, XN, times):
            with ExitStack() as c:
                S = Sems(nc, c, tag)
                st = sb(c, tag + "_stats", [P, NT, 6])
                mv = sb(c, tag + "_meanvar", [P, NT, 2])
                ve = sb(c, tag + "_vareps", [P, NT])
                rs = sb(c, tag + "_rstd", [P, NT])
                for k in range(times):
                    S(f"st{k}"), S(f"mv{k}"), S(f"ve{k}"), S(f"rs{k}"), S(f"xn{k}")
                block = c.enter_context(nc.Block())

                @block.vector
                def _(dve):
                    for k in range(times):
                        src = XR if k == 0 else XN
                        with dve.Fori(0, NT // 4) as i:
                            for j in range(4):
                                nc.vector.bn_stats(st[:, bass.ds(4 * i + j, 1), :].rearrange("p a b -> p (a b)"),
                                                   src[:, bass.ds(4 * i + j, 1), :].rearrange("p a b -> p (a b)")
                                                   ).then_inc(S(f"st{k}"), 1)
                        dve.wait_ge(S(f"st{k}"), NT)
                        for n in range(NT):
                            nc.vector.bn_aggr(mv[:, n, :], st[:, n, :]).then_inc(S(f"mv{k}"), 1)
                        dve.wait_ge(S(f"rs{k}"), 1)
                        with dve.Fori(0, NT // 4) as i:
                            for j in range(4):
                                t = 4 * i + j
                                nc.vector.tensor_scalar(XN[:, bass.ds(t, 1), :], src[:, bass.ds(t, 1), :],
                                                        mv[:, bass.ds(t, 1), 0], rs[:, bass.ds(t, 1)],
                                                        ALU.subtract, ALU.mult).then_inc(S(f"xn{k}"), 1)
                        dve.wait_ge(S(f"xn{k}"), NT)

                @block.gpsimd
                def _(pool):
                    for k in range(times):
                        pool.wait_ge(S(f"mv{k}"), NT)
                        nc.gpsimd.tensor_scalar(ve[:], mv[:, :, 1], LN_EPS, None, ALU.add).then_inc(S(f"ve{k}"), 1)
                        pool.wait_ge(S(f"ve{k}"), 1)
                        nc.gpsimd.tensor_tensor(rs[:], ve[:], mhalf[:], ALU.pow).then_inc(S(f"rs{k}"), 1)

        def ffn(tag, outer):
            with ExitStack() as c:
                comb = sb(c, tag + "_comb", [P, NT, E])
                with ExitStack() as c2:
                    XN = sb(c2, tag + "_XN", [P, NT, D])
                    ln_phase(tag + "ln", XN, 2)
                    LG = sb(c2, tag + "_logits", [P, NT, E])
                    rT = sb(c2, tag + "_routerT", [P, E])
                    w8 = sb(c2, tag + "_w8", [P, E])
                    nT = [sb(c2, f"{tag}_nT{q}", [P, L]) for q in range(2)]
                    XNs = [sb(c2, f"{tag}_XNs{q}", [P, JT, D]) for q in range(2)]
                    with ExitStack() as c3:
                        psT = [ps(c3, f"{tag}_psT{q}", [P, L]) for q in range(2)]
                        psL = [ps(c3, f"{tag}_psL{q}", [P, L]) for q in range(2)]
                        S = Sems(nc, c3, tag + "tr")
                        s_w, s_tp, s_nT, s_lg, s_lgc, s_st = (S(x) for x in ("w", "tp", "nT", "lg", "lgc", "st"))
                        block = c3.enter_context(nc.Block())
                        NB = NT // JT

                        @block.sync
                        def _(sp):
                            sp.dma_start(rT[:], T["routerT"]).then_inc(s_w, 16)
                            sp.dma_start(w8[:], T["w8"]).then_inc(s_w, 16)

                            def store(i, q):
                                done, stored = snapped(sp, i + 1, 16 * i)
                                sp.wait_ge(s_nT, done)
                                if not (isinstance(i, int) and i == 0):
                                    sp.wait_ge(s_st, stored)
                                sp.dma_start(xn_t[:, bass.ds(i * L, L)], nT[q][:]).then_inc(s_st, 16)

                            for q in range(2):
                                store(q, q)
                            with sp.Fori(1, NB // 2) as i2:
                                for q in range(2):
                                    store(i2 * 2 + q, q)
                            sp.wait_ge(s_w, 32)
                            sp.wait_ge(s_st, 16 * NB)

                        @block.tensor
                        def _(pe):
                            pe.wait_ge(s_w, 32)

                            def block_(i, q, first):
                                if not first:
                                    pe.wait_ge(s_nT, i - 1)
                                for j in range(JT):
                                    m = nc.tensor.transpose(psT[q][:, j * P:(j + 1) * P], XNs[q][:, j, :], ident[:])
                                m.then_inc(s_tp, 1)
                                pe.wait_ge(s_nT, i + 1)
                                if not first:
                                    pe.wait_ge(s_lgc, i - 1)
                                for j in range(JT):
                                    m = nc.tensor.matmul(psL[q][:, j * E:(j + 1) * E], nT[q][:, j * P:(j + 1) * P],
                                                         rT[:], start=True, stop=True)
                                m.then_inc(s_lg, 1)

                            for q in range(2):
                                pe.wait_ge(S("xs"), q + 1)
                                block_(q, q, True)
                            with pe.Fori(1, NB // 2) as i2:
                                for q in range(2):
                                    pe.wait_ge(S("xs"), i2 * 2 + q + 1)
                                    block_(i2 * 2 + q, q, False)

                        @block.vector
                        def _(dve):
                            def stage(i, q, first):
                                if not first:
                                    dve.wait_ge(s_tp, i - 1)
                                nc.vector.tensor_copy(XNs[q][:], XN[:, bass.ds(i * JT, JT), :]).then_inc(S("xs"), 1)

                            for q in range(2):
                                stage(q, q, True)
                            with dve.Fori(1, NB // 2) as i2:
                                for q in range(2):
                                    stage(i2 * 2 + q, q, False)

                        @block.scalar
                        def _(act):
                            def evac(i, q, first):
                                act.wait_ge(s_tp, i + 1)
                                if not first:
                                    act.wait_ge(s_st, 16 * (i - 1))
                                    act.wait_ge(s_lg, i - 1)
                                nc.scalar.activation(nT[q][:], psT[q][:], ACT.Identity, bias=bet[:], scale=gam[:]
                                                     ).then_inc(s_nT, 1)
                                act.wait_ge(s_lg, i + 1)
                                nc.scalar.activation(LG[:, bass.ds(i * JT, JT), :],
                                                     psL[q][:, 0:JT * E].rearrange("p (j e) -> p j e", e=E),
                                                     ACT.Copy).then_inc(s_lgc, 1)

                            for q in range(2):
                                evac(q, q, True)
                            with act.Fori(1, NB // 2) as i2:
                                for q in range(2):
                                    evac(i2 * 2 + q, q, False)

                    with ExitStack() as c3:
                        S = Sems(nc, c3, tag + "rt")
                        s_d, s_a = S("dve"), S("act")
                        a = sb(c3, tag + "_ra", [P, NT, E])
                        b_ = sb(c3, tag + "_rb", [P, NT, E])
                        s1 = sb(c3, tag + "_s1", [P, NT, E])
                        s2 = sb(c3, tag + "_s2", [P, NT, E])
                        v = sb(c3, tag + "_rv", [P, 8, NT])
                        block = c3.enter_context(nc.Block())

                        @block.vector
                        def _(dve):
                            n = [0]

                            def link(ins):
                                n[0] += 1
                                ins.then_inc(s_d, 1)
                                dve.wait_ge(s_d, n[0])

                            def bc(col):
                                return col.unsqueeze(2).broadcast_to([P, NT, E])

                            w8b = w8[:].unsqueeze(1).broadcast_to([P, NT, E])
                            tt, ts = nc.vector.tensor_tensor, nc.vector.tensor_scalar
                            link(nc.vector.reduce_max(v[:, 0, :], LG[:], AX))
                            link(tt(a[:], LG[:], bc(v[:, 0, :]), ALU.subtract))
                            dve.wait_ge(s_a, 1)
                            link(nc.vector.reduce_sum(v[:, 1, :], b_[:], AX))
                            link(nc.vector.reciprocal(v[:, 2, :], v[:, 1, :]))
                            link(tt(a[:], b_[:], bc(v[:, 2, :]), ALU.mult))

                            def pick(m, out):
                                link(nc.vector.reduce_max(m, a[:], AX))
                                link(tt(b_[:], a[:], bc(m), ALU.is_equal))
                                link(tt(b_[:], b_[:], w8b, ALU.mult))
                                link(nc.vector.reduce_max(v[:, 7, :], b_[:], AX))
                                link(tt(out, b_[:], bc(v[:, 7, :]), ALU.is_equal))

                            pick(v[:, 3, :], s1[:])
                            link(nc.vector.scalar_tensor_tensor(out=a[:], in0=s1[:], scalar=-2.0, in1=a[:],
                                                                op0=ALU.mult, op1=ALU.add))
                            pick(v[:, 4, :], s2[:])
                            link(tt(v[:, 5, :], v[:, 4, :], v[:, 3, :], ALU.subtract))
                            dve.wait_ge(s_a, 2)
                            link(ts(v[:, 0, :], v[:, 6, :], 1.0, None, ALU.add))
                            link(nc.vector.reciprocal(v[:, 1, :], v[:, 0, :]))
                            link(tt(v[:, 2, :], v[:, 1, :], v[:, 6, :], ALU.mult))
                            link(tt(a[:], s1[:], bc(v[:, 1, :]), ALU.mult))
                            link(tt(b_[:], s2[:], bc(v[:, 2, :]), ALU.mult))
                            link(tt(comb[:], a[:], b_[:], ALU.add))

                        @block.scalar
                        def _(act):
                            act.wait_ge(s_d, 2)
                            nc.scalar.activation(b_[:], a[:], ACT.Exp).then_inc(s_a, 1)
                            act.wait_ge(s_d, 5 + 5 + 1 + 5 + 1)
                            nc.scalar.activation(v[:, 6, :], v[:, 5, :], ACT.Exp).then_inc(s_a, 1)

                with ExitStack() as c3:
                    NC_ = 1 + E * FC
                    Wg = sb(c3, tag + "_Wg", [P, NC_, P])
                    Wu = sb(c3, tag + "_Wu", [P, NC_, P])
                    Wd = sb(c3, tag + "_Wd", [P, NC_, P])
                    nin = sb(c3, tag + "_nin", [P, L])
                    nT = sb(c3, tag + "_nTe", [P, L])
                    sg = [sb(c3, f"{tag}_sg{q}", [P, L]) for q in range(2)]
                    h = [sb(c3, f"{tag}_h{q}", [P, L]) for q in range(2)]
                    acc = sb(c3, tag + "_acc", [P, JT, D])
                    psG = [ps(c3, f"{tag}_psG{q}", [P, L]) for q in range(2)]
                    psU = [ps(c3, f"{tag}_psU{q}", [P, L]) for q in range(2)]
                    psD = [ps(c3, f"{tag}_psD{q}", [P, JT, D]) for q in range(2)]
                    S = Sems(nc, c3, tag + "ex")
                    s_w, s_ld, s_nT, s_gu, s_sg, s_h, s_dn, s_ac, s_x = (
                        S(x) for x in ("w", "ld", "nT", "gu", "sg", "h", "dn", "ac", "x"))
                    block = c3.enter_context(nc.Block())
                    expert_of = [0] + [1 + k // FC for k in range(E * FC)]
                    last_of = [k == NC_ - 1 or expert_of[k + 1] != expert_of[k] for k in range(NC_)]
                    first_of = [k == 0 or expert_of[k - 1] != expert_of[k] for k in range(NC_)]
                    NE = 1 + E

                    @block.sync
                    def _(sp):
                        sp.dma_start(Wg[:], T["WgT"]).then_inc(s_w, 16)
                        sp.dma_start(Wu[:], T["WuT"]).then_inc(s_w, 16)
                        sp.dma_start(Wd[:], T["WdT"]).then_inc(s_w, 16)
                        sp.dma_start(nin[:], xn_t[:, 0:L]).then_inc(s_ld, 16)
                        with sp.Fori(1, B) as i:
                            sp.wait_ge(s_nT, i)
                            sp.dma_start(nin[:], xn_t[:, bass.ds(i * L, L)]).then_inc(s_ld, 16)

                    @block.scalar
                    def _(act):
                        def blk(i, first):
                            act.wait_ge(s_ld, 16 * i + 16)
                            if not first:
                                act.wait_ge(s_gu, i * NC_)
                            nc.scalar.activation(nT[:], nin[:], ACT.Copy).then_inc(s_nT, 1)
                            for k in range(NC_):
                                act.wait_ge(s_gu, i * NC_ + k + 1)
                                if k >= 2 or not first:
                                    act.wait_ge(s_h, slot_free(i, NC_, k))
                                q = k % 2
                                nc.scalar.activation(sg[q][:], psG[q][:], ACT.Silu).then_inc(s_sg, 1)

                        blk(0, True)
                        with act.Fori(1, B) as i:
                            blk(i, False)

                    @block.vector
                    def _(dve):
                        def blk(i, first):
                            for k in range(NC_):
                                q = k % 2
                                dve.wait_ge(s_sg, i * NC_ + k + 1)
                                if k >= 2 or not first:
                                    dve.wait_ge(s_dn, slot_free(i, NC_, k))
                                nc.vector.tensor_tensor(h[q][:], psU[q][:], sg[q][:], ALU.mult).then_inc(s_h, 1)
                                if k >= 1 and last_of[k - 1]:
                                    add(i, expert_of[k - 1], k - 1)
                            add(i, NE - 1, NC_ - 1)
                            dve.wait_ge(s_ac, (i + 1) * NE * JT)
                            x = XR[:, bass.ds(i * JT, JT), :]
                            nc.vector.scalar_tensor_tensor(out=x, in0=acc[:], scalar=0.5, in1=x,
                                                           op0=ALU.mult, op1=ALU.add).then_inc(s_x, 1)
                            dve.wait_ge(s_x, i + 1)

                        def add(i, e, k):
                            dve.wait_ge(s_dn, i * NC_ + k + 1)
                            if e:
                                dve.wait_ge(s_ac, (i * NE + e) * JT)
                            for j in range(JT):
                                if e == 0:
                                    ins = nc.vector.tensor_copy(acc[:, j, :], psD[0][:, j, :])
                                else:
                                    ins = nc.vector.scalar_tensor_tensor(
                                        out=acc[:, j, :], in0=psD[e % 2][:, j, :],
                                        scalar=comb[:, bass.ds(i * JT + j, 1), e - 1], in1=acc[:, j, :],
                                        op0=ALU.mult, op1=ALU.add)
                                ins.then_inc(s_ac, 1)

                        blk(0, True)
                        with dve.Fori(1, B) as i:
                            blk(i, False)

                    @block.tensor
                    def _(pe):
                        pe.wait_ge(s_w, 48)

                        def blk(i, first):
                            pe.wait_ge(s_nT, i + 1)

                            def gate_up(k):
                                q = k % 2
                                if k >= 2 or not first:
                                    pe.wait_ge(s_h, slot_free(i, NC_, k))
                                nc.tensor.matmul(psG[q][:], Wg[:, k, :], nT[:], start=True, stop=True)
                                nc.tensor.matmul(psU[q][:], Wu[:, k, :], nT[:], start=True, stop=True).then_inc(s_gu, 1)

                            def down(k):
                                e = expert_of[k]
                                pe.wait_ge(s_h, i * NC_ + k + 1)
                                if first_of[k] and (e >= 2 or not first):
                                    pe.wait_ge(s_ac, slot_free(i, NE, e) * JT)
                                for j in range(JT):
                                    m = nc.tensor.matmul(psD[e % 2][:, j, :], h[k % 2][:, j * P:(j + 1) * P],
                                                         Wd[:, k, :], start=first_of[k] and j == 0, stop=last_of[k],
                                                         skip_group_check=True)
                                m.then_inc(s_dn, 1)

                            gate_up(0)
                            for k in range(NC_):
                                if k + 1 < NC_:
                                    gate_up(k + 1)
                                down(k)

                        blk(0, True)
                        with pe.Fori(1, B) as i:
                            blk(i, False)

        ffn("f1", top)
        attention(nc, T, top, sb, ps, XR, ident, rec, qd, rsd, otd, ln_phase)
        ffn("f2", top)

        with nc.semaphore("store_out") as s_out, nc.Block() as block:
            @block.sync
            def _(sp):
                ov = T["out"].rearrange("(n p) d -> p n d", p=P)
                for q in range(4):
                    sp.dma_start(ov[:, 16 * q:16 * q + 16, :], XR[:, 16 * q:16 * q + 16, :]).then_inc(s_out, 16)
                sp.wait_ge(s_out, 64)


def attention(nc, T, top, sb, ps, XR, ident, rec, qd, rsd, otd, ln_phase):
    tag = "at"
    with ExitStack() as c:
        XN = sb(c, "at_XN", [P, NT, D])
        ln_phase("atln", XN, 1)
        wq = sb(c, "at_WqT", [P, D])
        wk = sb(c, "at_WkT", [P, D])
        wv = sb(c, "at_WvT", [P, D])
        bq = sb(c, "at_bq", [P, 1])
        bk = sb(c, "at_bk", [P, 1])
        bks = sb(c, "at_bk_scaled", [P, 1])
        bv = sb(c, "at_bv", [P, 1])
        XNs = sb(c, "at_XNs", [P, JT, D])
        xT = sb(c, "at_xT", [P, L])
        Qf = sb(c, "at_Qf", [P, L])
        Kf = sb(c, "at_Kf", [P, L])
        Vf = sb(c, "at_Vf", [P, L])
        R = [sb(c, f"at_rec{q}", [P, REC], F32R) for q in range(2)]
        psT = ps(c, "at_psT", [P, L])
        psQ = [ps(c, f"at_psQ{q}", [P, L]) for q in range(3)]
        S = Sems(nc, c, "qkv")
        s_w, s_xs, s_tp, s_xT, s_mm, s_f, s_b, s_r, s_st = (
            S(x) for x in ("w", "xs", "tp", "xT", "mm", "f", "b", "r", "st"))
        isq = float(1.0 / np.sqrt(HD))
        block = c.enter_context(nc.Block())

        @block.sync
        def _(sp):
            for dst, src in ((wq, "WqT"), (wk, "WkT"), (wv, "WvT"), (bq, "bq"), (bk, "bk"), (bv, "bv")):
                sp.dma_start(dst[:], T[src]).then_inc(s_w, 16)
            sp.wait_ge(s_w, 96)

            def store(b, q, first):
                done, stored = snapped(sp, (b + 1) * 5, 48 * b)
                sp.wait_ge(s_r, done)
                if not first:
                    sp.wait_ge(s_st, stored)
                sp.dma_start(rec[bass.ds(b, 1), :, :].rearrange("a p n -> (a p) n"), R[q][:].bitcast(F32)
                             ).then_inc(s_st, 16)
                for part in range(2):
                    src = R[q][:, (2 + part) * L:(3 + part) * L].bitcast(F32).rearrange("p (a t) -> p a t", a=A8)
                    dst = qd[bass.ds(b, 1), part, :, :, :].rearrange("b a p t -> p (b a) t")
                    sp.dma_start(dst, src).then_inc(s_st, 16)

            store(0, 0, True)
            store(1, 1, False)
            with sp.Fori(1, B // 2) as b2:
                for q in range(2):
                    store(b2 * 2 + q, q, False)
            sp.wait_ge(s_st, 48 * B)

        @block.tensor
        def _(pe):
            pe.wait_ge(s_w, 96)

            def seq(b, first):
                pe.wait_ge(s_xs, b + 1)
                for j in range(JT):
                    m = nc.tensor.transpose(psT[:, j * P:(j + 1) * P], XNs[:, j, :], ident[:])
                m.then_inc(s_tp, 1)
                pe.wait_ge(s_xT, b + 1)
                if not first:
                    pe.wait_ge(s_f, b * 3)
                for n, w in enumerate((wq, wk, wv)):
                    nc.tensor.matmul(psQ[n][:], w[:], xT[:], start=True, stop=True).then_inc(s_mm, 1)

            seq(0, True)
            with pe.Fori(1, B) as b:
                seq(b, False)

        @block.scalar
        def _(act):
            act.wait_ge(s_w, 96)
            nc.scalar.activation(bks[:], bk[:], ACT.Copy, scale=isq).then_inc(s_b, 1)
            act.wait_ge(s_b, 1)

            def seq(b, first):
                act.wait_ge(s_tp, b + 1)
                if not first:
                    act.wait_ge(s_mm, b * 3)
                nc.scalar.activation(xT[:], psT[:], ACT.Copy).then_inc(s_xT, 1)
                if not first:
                    act.wait_ge(s_r, b * 5)
                for n, (dst, bias, scale) in enumerate(((Qf, bq, 1.0), (Kf, bks, isq), (Vf, bv, 1.0))):
                    act.wait_ge(s_mm, b * 3 + n + 1)
                    nc.scalar.activation(dst[:], psQ[n][:], ACT.Identity, bias=bias[:], scale=scale).then_inc(s_f, 1)

            seq(0, True)
            with act.Fori(1, B) as b:
                seq(b, False)

        @block.vector
        def _(dve):
            def seq(b, q, first):
                if first:
                    if b >= 1:
                        dve.wait_ge(s_tp, b)
                else:
                    dve.wait_ge(s_tp, b)
                    dve.wait_ge(s_st, 48 * (b - 1))
                nc.vector.tensor_copy(XNs[:], XN[:, bass.ds(b * JT, JT), :]).then_inc(s_xs, 1)
                r = R[q]
                for n, (src, at) in enumerate(((Qf, 2), (Kf, 0))):
                    dve.wait_ge(s_f, b * 3 + n + 1)
                    nc.vector.tensor_copy(r[:, at * L:(at + 1) * L], src[:]).then_inc(s_r, 1)
                    dve.wait_ge(s_r, b * 5 + 2 * n + 1)
                    nc.vector.tensor_tensor(r[:, (at + 1) * L:(at + 2) * L], src[:],
                                            r[:, at * L:(at + 1) * L].bitcast(F32), ALU.subtract).then_inc(s_r, 1)
                dve.wait_ge(s_f, b * 3 + 3)
                nc.vector.transpose(r[:, 4 * L:5 * L].bitcast(F32), Vf[:]).then_inc(s_r, 1)

            for q in range(2):
                seq(q, q, True)
            with dve.Fori(1, B // 2) as b2:
                for q in range(2):
                    seq(b2 * 2 + q, q, False)

    with ExitStack() as c:
        RA = sb(c, "rel_hi", [P, RELW], F32R)
        RB = sb(c, "rel_lo", [P, RELW], F32R)
        RF = sb(c, "rel_f32", [P, RELW])
        maskh = sb(c, "mask_head", [P, H])
        maska = sb(c, "mask_a", [P, A8])
        KQ = sb(c, "record_ring", [P, 2, REC], F32R)
        M0 = sb(c, "q_by_query_ring", [P, 2, H, NQ])
        NS = 8
        SQ = [sb(c, f"stat_q{s}", [P, 2, H, A8], F32R) for s in range(NS)]
        SR = [sb(c, f"stat_r{s}", [P, H, A8], F32R) for s in range(NS)]
        nmx = sb(c, "neg_max", [P, 4])
        Pr = [sb(c, f"probs{s}", [P, L]) for s in range(4)]
        PT = [sb(c, f"probs_T{s}", [P, KEYS32, 4, GT, A8]) for s in range(2)]
        W = sb(c, "values_diag", [P, 4, KEYS32, 4, HD])
        rs = sb(c, "row_sum", [P, 2, GT])
        rb = sb(c, "row_sum_T", [P, 2, A8, GT])
        ri = sb(c, "recip_sum", [P, A8, GT])
        OT = sb(c, "attn_out", [P, A8, NQ])
        psS = [ps(c, f"ps_scores{s}", [P, L]) for s in range(4)]
        psO = [ps(c, f"ps_out{s}", [P, GT, A8]) for s in range(2)]
        S = Sems(nc, c, "att")
        (s_rf, s_rh, s_rec, s_m0, s_ex, s_sc, s_mx, s_p, s_tr, s_wz, s_we, s_pv, s_rs, s_rb, s_ri, s_o, s_ot, s_mk) = (
            S(x) for x in ("relf", "rel", "rec", "m0", "expanded", "scores", "max", "probs", "transposed", "wzero",
                           "wexp", "pv", "rsum_out", "rsum_in", "recip", "out", "out_st", "masks"))
        block = c.enter_context(nc.Block())

        @block.sync
        def _(sp):
            for part in range(2):
                for a in range(A8):
                    p0 = part * 64 + a * HD
                    off = L - 1 - (NQ - 1) - NQ * a
                    sp.dma_start(RF[p0:p0 + HD, :], T["relT"][:, off:off + RELW]).then_inc(s_rf, 16)
            sp.dma_start(maskh[:], T["maskh"]).then_inc(s_mk, 16)
            sp.dma_start(maska[:], T["maska"]).then_inc(s_mk, 16)

            def load(b, par):
                sp.dma_start(KQ[:, bass.ds(par, 1), :].rearrange("p o n -> p (o n)").bitcast(F32),
                             rec[bass.ds(b, 1), :, :].rearrange("a p n -> (a p) n")).then_inc(s_rec, 16)
                for part in range(2):
                    for a in range(A8):
                        p0 = part * 64 + a * HD
                        src = qd[bass.ds(b, 1), part, a, :, :].rearrange("b (h d) t -> d (b h) t", d=HD)
                        sp.dma_start(M0[p0:p0 + HD, bass.ds(par, 1), :, :].rearrange("p o h t -> p (o h) t"), src
                                     ).then_inc(s_m0, 16)

            def seq(b, first, last):
                ahead, n_rec, n_m0, n_o, n_sc, n_we = snapped(
                    sp, (b + 1) % 2, 16 * (b + 1), 256 * (b + 1), b * NG, b * NQ, 4 * b)
                sp.wait_ge(s_rec, n_rec)
                sp.wait_ge(s_m0, n_m0)
                for g in range(NG):
                    G = b * NG + g
                    n_p, n_rs, n_ri, n_rb = snapped(sp, (G + 1) * GT, 16 * (G + 1), G - 1, 64 * G)
                    sp.wait_ge(s_p, n_p)
                    sp.dma_start(rsd[bass.ds(G, 1), :, :].rearrange("o p t -> (o p) t"), rs[:, g % 2, :]
                                 ).then_inc(s_rs, 16)
                    sp.wait_ge(s_rs, n_rs)
                    if not (first and g < 2):
                        sp.wait_ge(s_ri, n_ri)
                    if not (first and g == 0):
                        sp.wait_ge(s_rb, n_rb)
                    for hh in range(4):
                        src = rsd[bass.ds(G, 1), :, :].rearrange("o (k hh a) t -> hh (o k) (a t)", k=4, hh=4)[hh]
                        src = src.unsqueeze(1).broadcast_to([4, HD, A8 * GT])
                        dst = rb[32 * hh:32 * hh + 32, g % 2, :, :].rearrange("p a t -> p (a t)")
                        sp.dma_start(dst, src).then_inc(s_rb, 16)
                    if g == 0 and not first:
                        sp.wait_ge(s_o, n_o)
                        sp.dma_start(otd[bass.ds(b - 1, 1), :, :].rearrange("a p n -> (a p) n"),
                                     OT[:].rearrange("p a t -> p (a t)")).then_inc(s_ot, 16)
                    if g == 1 and not last:
                        if not first:
                            sp.wait_ge(s_sc, n_sc)
                            sp.wait_ge(s_we, n_we)
                        load(b + 1, ahead)

            load(0, 0)
            seq(0, True, False)
            with sp.Fori(1, B - 1) as b:
                seq(b, False, False)
            seq(B - 1, False, True)
            sp.wait_ge(s_o, B * NG)
            sp.dma_start(otd[B - 1], OT[:].rearrange("p a t -> p (a t)")).then_inc(s_ot, 16)
            sp.wait_ge(s_ot, 16 * B)

        @block.gpsimd
        def _(pool):
            pool.wait_ge(s_mk, 32)
            mh = maskh[:].unsqueeze(2).broadcast_to([P, H, A8]).unsqueeze(1).broadcast_to([P, 2, H, A8])
            ma = maska[:].unsqueeze(1).broadcast_to([P, H, A8])

            def seq(b, first):
                pool.wait_ge(s_rec, 16 * (b + 1))
                pool.wait_ge(s_m0, 256 * (b + 1))
                par = b % 2
                for t in range(NQ):
                    n = b * NQ + t
                    s = t % NS
                    if not (first and t < NS):
                        pool.wait_ge(s_sc, n - NS + 1)
                    q = KQ[:, bass.ds(par, 1), 2 * L:4 * L].bitcast(F32).rearrange(
                        "p o (c a t) -> p (o c) a t", c=2, a=A8)[:, :, :, t]
                    q = q.unsqueeze(2).broadcast_to([P, 2, H, A8])
                    nc.gpsimd.tensor_tensor(SQ[s][:], q, mh, ALU.mult).then_inc(s_ex, 1)
                    m0 = M0[:, bass.ds(par, 1), :, t].rearrange("p o h -> p (o h)")
                    nc.gpsimd.tensor_tensor(SR[s][:], m0.unsqueeze(2).broadcast_to([P, H, A8]), ma, ALU.mult
                                            ).then_inc(s_ex, 1)

            seq(0, True)
            with pool.Fori(1, B) as b:
                seq(b, False)

        @block.tensor
        def _(pe):
            pe.wait_ge(s_rh, 2)

            def values(G, par, first2):
                pe.wait_ge(s_tr, (G + 1) * GT)
                if not first2:
                    pe.wait_ge(s_o, G - 1)
                for r in range(KEYS32):
                    for hh in range(4):
                        m = nc.tensor.matmul(psO[par][32 * hh:32 * hh + 32, :, :].rearrange("p t a -> p (t a)"),
                                             W[:, hh, r, :, :].rearrange("p k d -> p (k d)"),
                                             PT[par][:, r, hh, :, :].rearrange("p t a -> p (t a)"),
                                             start=(r == 0), stop=(r == KEYS32 - 1))
                m.then_inc(s_pv, 1)

            def seq(b, first):
                pe.wait_ge(s_rec, 16 * (b + 1))
                par = b % 2
                for t in range(NQ):
                    n = b * NQ + t
                    s, bank = t % NS, t % 4
                    pe.wait_ge(s_ex, 2 * (n + 1))
                    if not (first and t < 4):
                        pe.wait_ge(s_p, n - 3)
                    khi = KQ[:, bass.ds(par, 1), 0:L].rearrange("p o n -> p (o n)")
                    klo = KQ[:, bass.ds(par, 1), L:2 * L].rearrange("p o n -> p (o n)")
                    qh = SQ[s][:, 0, :, :].rearrange("p h a -> p (h a)")
                    ql = SQ[s][:, 1, :, :].rearrange("p h a -> p (h a)")
                    qr = SR[s][:].rearrange("p h a -> p (h a)")
                    w0 = NQ - 1 - t
                    nc.tensor.matmul(psS[bank][:], qr, RA[:, w0:w0 + L], start=True, stop=False)
                    nc.tensor.matmul(psS[bank][:], qr, RB[:, w0:w0 + L], start=False, stop=False)
                    nc.tensor.matmul(psS[bank][:], qh, khi, start=False, stop=False)
                    nc.tensor.matmul(psS[bank][:], qh, klo, start=False, stop=False)
                    nc.tensor.matmul(psS[bank][:], ql, khi, start=False, stop=True).then_inc(s_sc, 1)
                    if t % GT == 3 and not (first and t == 3):
                        g = t // GT
                        if g == 1:
                            pe.wait_ge(s_we, 4 * (b + 1))
                        values(b * NG + g - 1, (g - 1) % 2, first and g < 3)

            seq(0, True)
            with pe.Fori(1, B) as b:
                seq(b, False)
            values(B * NG - 1, 1, False)

        @block.vector
        def _(dve):
            nc.vector.memset(W[:], 0.0).then_inc(s_wz, 1)
            dve.wait_ge(s_rf, 256)
            nc.vector.tensor_copy(RA[:], RF[:]).then_inc(s_rh, 1)
            dve.wait_ge(s_rh, 1)
            nc.vector.tensor_tensor(RB[:], RF[:], RA[:].bitcast(F32), ALU.subtract).then_inc(s_rh, 1)

            def transpose(b, t, first):
                dve.wait_ge(s_p, b * NQ + t + 1)
                g, tt = t // GT, t % GT
                if tt == 0 and not (first and g < 2):
                    dve.wait_ge(s_pv, b * NG + g - 1)
                nc.vector.transpose(PT[g % 2][:, :, :, tt, :],
                                    Pr[t % 4][:].rearrange("p (r x) -> p r x", x=32)).then_inc(s_tr, 1)

            def norm(G, g, first2, b):
                dve.wait_ge(s_rb, 64 * (G + 1))
                if not (first2 and g == 0):
                    dve.wait_ge(s_o, G)
                nc.vector.reciprocal(ri[:], rb[:, g % 2, :, :]).then_inc(s_ri, 1)
                dve.wait_ge(s_ri, G + 1)
                dve.wait_ge(s_pv, G + 1)
                if g == 0 and not first2:
                    dve.wait_ge(s_ot, 16 * b)
                nc.vector.tensor_tensor(OT[:, :, g * GT:(g + 1) * GT].rearrange("p a t -> p t a"), psO[g % 2][:],
                                        ri[:].rearrange("p a t -> p t a"), ALU.mult).then_inc(s_o, 1)

            def seq(b, first):
                for t in range(NQ):
                    n = b * NQ + t
                    dve.wait_ge(s_sc, n + 1)
                    if not (first and t < 4):
                        dve.wait_ge(s_p, n - 3)
                    nc.vector.reduce_max(nmx[:, t % 4:t % 4 + 1], psS[t % 4][:], AX, negate=True).then_inc(s_mx, 1)
                    if t >= 1:
                        transpose(b, t - 1, first)
                    elif not first:
                        transpose(b - 1, NQ - 1, False)
                    if t % GT == 8 and not (first and t == 8):
                        g = t // GT
                        if g == 0:
                            norm(b * NG - 1, 3, False, b - 1)
                        else:
                            norm(b * NG + g - 1, g - 1, first, b)

            seq(0, True)
            with dve.Fori(1, B) as b:
                seq(b, False)
            transpose(B - 1, NQ - 1, False)
            norm(B * NG - 1, 3, False, B - 1)

        @block.scalar
        def _(act):
            def seq(b, first):
                for t in range(NQ):
                    n = b * NQ + t
                    g, tt = t // GT, t % GT
                    act.wait_ge(s_mx, n + 1)
                    if not (first and t < 4):
                        act.wait_ge(s_tr, n - 3)
                    if tt == 0 and not (first and g < 2):
                        act.wait_ge(s_rs, 16 * (b * NG + g - 1))
                    nc.scalar.activation(Pr[t % 4][:], psS[t % 4][:], ACT.Exp, bias=nmx[:, t % 4:t % 4 + 1],
                                         accum_out=rs[:, g % 2, tt:tt + 1]).then_inc(s_p, 1)
                    if t == 10:
                        if first:
                            act.wait_ge(s_wz, 1)
                        else:
                            act.wait_ge(s_pv, b * NG)
                        act.wait_ge(s_rec, 16 * (b + 1))
                        for k in range(4):
                            p = slice(32 * k, 32 * k + 32)
                            src = KQ[p, bass.ds(b % 2, 1), 4 * L:5 * L].bitcast(F32).rearrange(
                                "p o (r hh d) -> p (o hh) r d", hh=4, d=HD)
                            nc.scalar.activation(W[p, :, :, k, :], src, ACT.Copy).then_inc(s_we, 1)

            seq(0, True)
            with act.Fori(1, B) as b:
                seq(b, False)

    with ExitStack() as c:
        wo = sb(c, "at_WoT", [P, D])
        bo = sb(c, "at_bo", [P, D])
        Os = [sb(c, f"at_Os{q}", [P, L]) for q in range(2)]
        yo = sb(c, "at_y", [P, JT, D])
        psE = [ps(c, f"at_psE{q}", [P, JT, D]) for q in range(2)]
        S = Sems(nc, c, "oproj")
        s_w, s_ld, s_mm, s_y, s_x = (S(x) for x in ("w", "ld", "mm", "y", "x"))
        block = c.enter_context(nc.Block())

        @block.sync
        def _(sp):
            sp.dma_start(wo[:], T["WoT"]).then_inc(s_w, 16)
            sp.dma_start(bo[:], T["bo"].broadcast_to([P, D])).then_inc(s_w, 16)

            def load(b, q):
                sp.dma_start(Os[q][:], otd[bass.ds(b, 1), :, :].rearrange("a p n -> (a p) n")).then_inc(s_ld, 16)
            for q in range(2):
                if q:
                    sp.wait_ge(s_ld, 16)
                load(q, q)
            with sp.Fori(1, B // 2) as b2:
                for q in range(2):
                    b = b2 * 2 + q
                    used, loaded = snapped(sp, b - 1, 16 * b)
                    sp.wait_ge(s_mm, used)
                    sp.wait_ge(s_ld, loaded)
                    load(b, q)

        @block.tensor
        def _(pe):
            pe.wait_ge(s_w, 32)

            def seq(b, q, first):
                pe.wait_ge(s_ld, 16 * (b + 1))
                if not first:
                    pe.wait_ge(s_y, b - 1)
                for j in range(JT):
                    m = nc.tensor.matmul(psE[q][:, j, :], Os[q][:, j * P:(j + 1) * P], wo[:], start=True, stop=True)
                m.then_inc(s_mm, 1)
            for q in range(2):
                seq(q, q, True)
            with pe.Fori(1, B // 2) as b2:
                for q in range(2):
                    seq(b2 * 2 + q, q, False)

        @block.vector
        def _(dve):
            dve.wait_ge(s_w, 32)
            with dve.Fori(0, B // 2) as b2:
                for q in range(2):
                    b = b2 * 2 + q
                    dve.wait_ge(s_mm, b + 1)
                    nc.vector.tensor_tensor(yo[:], psE[q][:], bo[:].unsqueeze(1).broadcast_to([P, JT, D]), ALU.add
                                            ).then_inc(s_y, 1)
                    dve.wait_ge(s_y, b + 1)
                    x = XR[:, bass.ds(b * JT, JT), :]
                    nc.vector.tensor_tensor(x, x, yo[:], ALU.add).then_inc(s_x, 1)
                    dve.wait_ge(s_x, b + 1)


_F = np.float32


def kernel(**inputs):
    import concourse.bacc as _bacc
    from concourse.bass_utils import run_bass_kernel_spmd as _run

    a = {k[3:]: np.asarray(v) for k, v in inputs.items()}
    gu, dn = a["ffn_gate_up_w"], a["ffn_down_w"]
    sgu, sdn = a["ffn_shared_gate_up_w"], a["ffn_shared_down_w"]

    def chunks(shared, routed):
        return np.concatenate([shared, routed.reshape(E * FF, D)]).reshape(1 + E * FC, P, D).transpose(2, 0, 1)

    down = np.concatenate([sdn.T, dn.transpose(0, 2, 1).reshape(E * FF, D)]).reshape(1 + E * FC, P, D)
    rel = a["attn_rel_emb"]
    rel = np.concatenate([rel[MAXLEN - 1:], rel, np.repeat(rel[-1:], L - 1 - (MAXLEN - 1), axis=0)])
    arrays = {
        "x": a["attn_x"].reshape(TOK, D),
        "ident": np.eye(P, dtype=_F),
        "w8": np.broadcast_to(np.arange(E, 0, -1, dtype=_F), (P, E)),
        "maskh": np.kron(np.eye(H, dtype=_F), np.ones((HD, 1), _F)),
        "maska": np.concatenate([np.kron(np.eye(A8, dtype=_F), np.ones((HD, 1), _F))] * 2),
        "gamma": a["ffn_ln_gamma"].reshape(D, 1),
        "beta": a["ffn_ln_beta"].reshape(D, 1),
        "routerT": a["ffn_router_w"].T,
        "WgT": chunks(sgu[:SFF], gu[:, :FF]),
        "WuT": chunks(sgu[SFF:], gu[:, FF:]),
        "WdT": down.transpose(1, 0, 2),
        "WqT": a["attn_Wq"].T, "WkT": a["attn_Wk"].T, "WvT": a["attn_Wv"].T,
        "bq": a["attn_bq"].reshape(D, 1), "bk": a["attn_bk"].reshape(D, 1), "bv": a["attn_bv"].reshape(D, 1),
        "WoT": a["attn_Wo"].T.reshape(4, 4, HD, D).transpose(1, 0, 2, 3).reshape(D, D),
        "bo": a["attn_bo"].reshape(1, D),
        "relT": rel.T,
    }
    arrays = {f"in_{k}": np.ascontiguousarray(v) for k, v in arrays.items()}
    nc = _bacc.Bacc("TRN2", target_bir_lowering=False, num_devices=1)
    T = {k[3:]: nc.dram_tensor(k, v.shape, F32, kind="ExternalInput").ap() for k, v in arrays.items()}
    T["out"] = nc.dram_tensor("out", (TOK, D), F32, kind="ExternalOutput").ap()
    build(nc, T)
    r = _run(nc, [arrays], core_ids=[0])
    return r.results[0]["out"].reshape(B, L, D)
```

```python
from contextlib import ExitStack

import numpy as np

import concourse.bass as bass
from concourse import mybir

F32 = mybir.dt.float32
F32R = mybir.dt.float32r
I32 = mybir.dt.int32
U32 = mybir.dt.uint32
ALU = mybir.AluOpType
ACT = mybir.ActivationFunctionType
AX = mybir.AxisListType.X

P = 128
D = 128
B, L = 16, 512
TOK = B * L
NT = TOK // P
JT = L // P
NB = NT // JT
E, FF, SFF = 8, 384, 128
TOPK = 2
FC = FF // P
REG = TOK + P
ET = (TOPK * TOK) // P + E
H, HD = 16, 8
MAXLEN = 256
LN_EPS = 1e-5
A8 = 8
NQ = L // A8
GT = 16
NG = NQ // GT
RELW = L + NQ - 1
KEYS32 = L // 32
REC = 2 * L + 2 * L + L


class Sems:

    def __init__(self, nc, ctx, prefix):
        self.nc, self.ctx, self.prefix, self.made = nc, ctx, prefix, {}

    def __call__(self, name):
        if name not in self.made:
            self.made[name] = self.ctx.enter_context(self.nc.semaphore(f"{self.prefix}_{name}"))
        return self.made[name]


def wait(eng, *pairs):
    pairs = [(s, v) for s, v in pairs if not (isinstance(v, int) and v <= 0)]
    for _, v in pairs:
        if not isinstance(v, int):
            eng.compute_val(v)
    for s, v in pairs:
        eng.wait_ge(s, v)


class Step:

    def __init__(self, lap, r):
        self.i, self.r = lap, r

    def n(self, off=0):
        return self.i * 4 + (self.r + off)

    def slot(self, off=0, ring=4):
        return (self.r + off) % ring

    def lap(self, off=0):
        return self.i + (self.r + off) // 4

    def on(self, off, count):
        return not isinstance(self.i, int) or 0 <= self.n(off) < count


def run_steps(eng, first, last, loop_from, loop_to, emit):
    for s in range(first, loop_from):
        emit(Step(s // 4, s % 4))
    with eng.Fori(loop_from // 4, loop_to // 4) as i:
        for r in range(4):
            emit(Step(i, r))
    for s in range(loop_to, last):
        emit(Step(s // 4, s % 4))


class Chain:

    def __init__(self, eng, sem, base):
        self.eng, self.sem, self.base, self.k = eng, sem, base, 0

    def __call__(self, ins, hold=True):
        ins.then_inc(self.sem, 1)
        self.k += 1
        if hold:
            wait(self.eng, (self.sem, self.base + self.k))


def flat(ap):
    return ap.rearrange("p a b -> p (a b)")


def build(nc, T):
    with ExitStack() as top:
        def sb(ctx, name, shape, dt=F32):
            return ctx.enter_context(nc.sbuf_tensor(name, shape, dt))

        def ps(ctx, name, shape):
            return ctx.enter_context(nc.psum_tensor(name, shape, F32))

        def dram(name, shape):
            return nc.dram_tensor(name, shape, F32).ap()

        XR = sb(top, "residual", [P, NT, D])
        ident = sb(top, "ident", [P, P])
        mhalf = sb(top, "minus_half", [P, JT])
        eps = sb(top, "eps", [P, JT])
        k1e = sb(top, "one_plus_eps", [P, JT])
        ke2 = sb(top, "eps_squared", [P, JT])
        gam = sb(top, "gamma_col", [P, 1])
        bet = sb(top, "beta_col", [P, 1])

        xd = dram("dispatched", [E * REG, D])
        yd = dram("expert_out", [ET * P, D])
        rec = dram("qkv_record", [B, P, REC])
        qd = dram("q_by_query", [B, 2, A8, P, NQ])
        rsd = dram("row_sums", [B * NG, P, GT])
        otd = dram("attn_out_T", [B, P, L])
        K = dict(nc=nc, T=T, sb=sb, ps=ps, XR=XR, ident=ident, mhalf=mhalf, eps=eps, k1e=k1e, ke2=ke2, gam=gam, bet=bet, xd=xd, yd=yd,
                 rec=rec, qd=qd, rsd=rsd, otd=otd)

        with nc.semaphore("load_in") as s_in, nc.semaphore("load_c") as s_c, nc.Block() as block:
            @block.sync
            def _(sp):
                xv = T["x"].rearrange("(n p) d -> p n d", p=P)
                for q in range(4):
                    sp.dma_start(XR[:, 16 * q:16 * q + 16, :], xv[:, 16 * q:16 * q + 16, :]).then_inc(s_in, 16)
                sp.wait_ge(s_in, 64)

            @block.scalar
            def _(act):
                act.dma_start(ident[:], T["ident"]).then_inc(s_c, 16)
                act.dma_start(gam[:], T["gamma"]).then_inc(s_c, 16)
                act.dma_start(bet[:], T["beta"]).then_inc(s_c, 16)
                act.wait_ge(s_c, 48)

            @block.vector
            def _(dve):
                for dst, value in ((mhalf, -0.5), (eps, LN_EPS), (k1e, 1.0 + LN_EPS), (ke2, LN_EPS * LN_EPS)):
                    nc.vector.memset(dst[:], value)

        ffn(K, "f1", False)
        attention(K)
        ffn(K, "f2", True)


def ffn(K, tag, last):
    nc, sb = K["nc"], K["sb"]
    with ExitStack() as c:
        R = dict(
            S1=sb(c, tag + "_pick1", [P, NT, E]),
            S2=sb(c, tag + "_pick2", [P, NT, E]),
            P1=sb(c, tag + "_row1", [P, NT]),
            P2=sb(c, tag + "_row2", [P, NT]),
            DD=sb(c, tag + "_pdiff", [P, NT]),
            Y1=sb(c, tag + "_yrow1", [P, NT], U32),
            Y2=sb(c, tag + "_yrow2", [P, NT], U32),
            G1=sb(c, tag + "_gate1", [P, NT]),
            G2=sb(c, tag + "_gate2", [P, NT]),
            run=sb(c, tag + "_fill", [P, E]),
            tab=sb(c, tag + "_tiletab", [1, 2, ET], I32),
            Wh=sb(c, tag + "_Wgu_hi", [P, E * 2 * FF], F32R),
            Wl=sb(c, tag + "_Wgu_lo", [P, E * 2 * FF], F32R),
            Wd=sb(c, tag + "_Wd", [P, E * FC, P]),
        )
        dispatch(K, tag, R, last)
        tile_map(K, tag, R)
        experts(K, tag, R)
        combine(K, tag, R, last)


def dispatch(K, tag, R, add_attention):
    nc, T, sb, ps, XR, ident, gam, bet, mhalf, k1e, ke2, xd = (
        K[k] for k in ("nc", "T", "sb", "ps", "XR", "ident", "gam", "bet", "mhalf", "k1e", "ke2", "xd"))
    S1, S2, P1, P2, DD, run, Wh, Wl, Wd = (R[k] for k in ("S1", "S2", "P1", "P2", "DD", "run", "Wh", "Wl", "Wd"))
    tag = tag + "d"
    WCH = E * 2 * FF // NB
    with ExitStack() as c:
        Wf = sb(c, tag + "_Wgu", [P, E * 2 * FF])
        rT = sb(c, tag + "_routerT", [P, E])
        w8 = sb(c, tag + "_w8", [P, E])
        erow = sb(c, tag + "_erow", [P, E])
        tri = sb(c, tag + "_tri", [P, P])
        ones = sb(c, tag + "_ones", [P, P])
        sgT = sb(c, tag + "_shG", [P, SFF])
        suT = sb(c, tag + "_shU", [P, SFF])
        sdT = sb(c, tag + "_shD", [P, D])
        st = sb(c, tag + "_stats", [P, JT, 6])
        mv = [sb(c, f"{tag}_mv{q}", [P, JT, 2]) for q in range(4)]
        ve = sb(c, tag + "_ve", [P, JT])
        vf = sb(c, tag + "_vf", [P, JT])
        rs = [sb(c, f"{tag}_rs{q}", [P, JT]) for q in range(4)]
        n0 = [sb(c, f"{tag}_n0{q}", [P, JT, D]) for q in range(4)]
        nT = [sb(c, f"{tag}_nT{q}", [P, L]) for q in range(2)]
        z = sb(c, tag + "_z", [P, JT, E])
        ez = sb(c, tag + "_ez", [P, JT, E])
        pr = sb(c, tag + "_pr", [P, JT, E])
        eq = sb(c, tag + "_eq", [P, JT, E])
        M = [sb(c, f"{tag}_M{q}", [P, JT, E]) for q in range(2)]
        v = sb(c, tag + "_v", [P, 8, JT])
        po = sb(c, tag + "_po", [P, JT, E])
        idx = [sb(c, f"{tag}_idx{q}", [P, TOPK, JT], U32) for q in range(4)]
        sg = [sb(c, f"{tag}_sg{q}", [P, L]) for q in range(2)]
        h = [sb(c, f"{tag}_h{q}", [P, L]) for q in range(2)]
        psT = ps(c, tag + "_psT", [P, L])
        psL = [ps(c, f"{tag}_psL{q}", [P, L]) for q in range(2)]
        psR = ps(c, tag + "_psR", [P, L])
        psG = ps(c, tag + "_psG", [P, L])
        psU = ps(c, tag + "_psU", [P, L])
        psY = ps(c, tag + "_psY", [P, JT, D])
        if add_attention:
            psE = ps(c, tag + "_psE", [P, JT, D])
            wo = sb(c, tag + "_WoT", [P, D])
            bo = sb(c, tag + "_bo", [1, D])
            Os = [sb(c, f"{tag}_Os{q}", [P, L]) for q in range(4)]
        S = Sems(nc, c, tag)
        s_w, s_wf, s_A, s_rs, s_C, s_tp, s_nT, s_lg, s_D, s_ex, s_rk, s_E, s_gu, s_sg, s_h, s_dn, s_add, s_hi, s_lo = (
            S(x) for x in ("w", "wf", "stats", "rstd", "normed", "transp", "nT", "logits", "route", "exp", "rank",
                           "rows", "gateup", "silu", "hidden", "down", "added", "whi", "wlo"))
        s_sc = [S(f"scattered{q}") for q in range(4)]
        if add_attention:
            s_os = [S(f"attn_in{q}") for q in range(4)]
            s_o, s_oa = S("oproj"), S("oadded")
        KA, KD, KE = 8, 18, 10
        NW = 9 + 2 * add_attention
        block = c.enter_context(nc.Block())

        @block.sync
        def _(sp):
            for dst, src in ((rT, "routerT"), (w8, "w8"), (erow, "erow"), (tri, "tri"), (ones, "ones"),
                             (sgT, "shG"), (suT, "shU"), (sdT, "shD")):
                sp.dma_start(dst[:], T[src]).then_inc(s_w, 16)
            sp.dma_start(run[:], T["erow"]).then_inc(s_w, 16)
            if add_attention:
                sp.dma_start(wo[:], T["WoT"]).then_inc(s_w, 16)
                sp.dma_start(bo[:], T["bo"]).then_inc(s_w, 16)
            sp.dma_start(Wf[:], T["WguT"]).then_inc(s_wf, 16)
            sp.dma_start(Wd[:], T["WdT"]).then_inc(s_wf, 16)
            if add_attention:
                def emit(st_):
                    if st_.on(0, NB):
                        wait(sp, (s_o, st_.n(-3)))
                        sp.dma_start(Os[st_.slot()][:], K["otd"][bass.ds(st_.n(), 1), :, :].rearrange(
                            "a p n -> (a p) n")).then_inc(s_os[st_.slot()], 16)
                run_steps(sp, 0, NB, 4, NB, emit)
            sp.wait_ge(s_wf, 32)

        @block.gpsimd
        def _(pool):
            tt = nc.gpsimd.tensor_tensor

            def emit(s):
                if s.on(0, NB):
                    wait(pool, (s_A, KA * s.n(1)), (s_E, KE * s.n(-1)))
                    tt(ve[:], mv[s.slot()][:, :, 1], k1e[:], ALU.mult).then_inc(s_rs, 1)
                    wait(pool, (s_rs, 3 * s.n() + 1))
                    tt(vf[:], ve[:], ke2[:], ALU.add).then_inc(s_rs, 1)
                    wait(pool, (s_rs, 3 * s.n() + 2), (s_C, JT * s.n(-3)))
                    tt(rs[s.slot()][:], vf[:], mhalf[:], ALU.pow).then_inc(s_rs, 1)
                elif s.on(-2, NB):
                    wait(pool, (s_E, KE * s.n(-1)))
                if s.on(-2, NB):
                    q = s.slot(-2)
                    for j in range(JT):
                        for k in range(TOPK):
                            pool.indirect_dma_start(xd, bass.IndirectOffsetOnAxis(idx[q][:, k, j:j + 1], 0),
                                                    n0[q][:, j, :], None).then_inc(s_sc[q], 16)
            run_steps(pool, 0, NB + 2, 4, NB, emit)
            for q in range(4):
                pool.wait_ge(s_sc[q], 16 * TOPK * JT * (NB // 4))

        @block.vector
        def _(dve):
            dve.wait_ge(s_w, 16 * NW)
            tt = nc.vector.tensor_tensor

            def bc(col):
                return col.unsqueeze(2).broadcast_to([P, JT, E])

            w8b = w8[:].unsqueeze(1).broadcast_to([P, JT, E])

            def emit(s):
                if add_attention and s.on(0, NB):
                    x = XR[:, bass.ds(JT * s.n(), JT), :]
                    wait(dve, (s_o, s.n(1)))
                    tt(x, x, psE[:], ALU.add).then_inc(s_oa, 1)
                    wait(dve, (s_oa, s.n(1)))
                if s.on(0, NB):
                    wait(dve, (s_A, KA * s.n()))
                if s.on(-2, NB):
                    ch = Chain(dve, s_D, KD * s.n(-2))
                    lg = psL[s.slot(-2, 2)][:, 0:JT * E].rearrange("p (j e) -> p j e", e=E)
                    wait(dve, (s_lg, s.n(-1)))
                    ch(nc.vector.reduce_max(v[:, 0, :], lg, AX))
                    ch(tt(z[:], lg, bc(v[:, 0, :]), ALU.subtract), hold=False)
                if s.on(0, NB):
                    ca = Chain(dve, s_A, KA * s.n())
                    for j in range(JT):
                        ca(nc.vector.bn_stats(st[:, j, :], flat(XR[:, bass.ds(JT * s.n() + j, 1), :])), hold=False)
                    wait(dve, (s_A, KA * s.n() + JT))
                if s.on(-2, NB):
                    blk = bass.ds(JT * s.n(-2), JT)
                    s1, s2, m1 = S1[:, blk, :], S2[:, blk, :], v[:, 3, :]
                    wait(dve, (s_ex, s.n(-1)))
                    ch(nc.vector.reduce_sum(v[:, 1, :], ez[:], AX), hold=False)
                if s.on(0, NB):
                    for j in range(JT):
                        ca(nc.vector.bn_aggr(mv[s.slot()][:, j, :], st[:, j, :]), hold=False)
                if s.on(-2, NB):
                    wait(dve, (s_D, KD * s.n(-2) + 3))
                    ch(nc.vector.reciprocal(v[:, 2, :], v[:, 1, :]))
                    ch(tt(pr[:], ez[:], bc(v[:, 2, :]), ALU.mult))

                    def pick(m, out):
                        ch(nc.vector.reduce_max(m, pr[:], AX))
                        ch(tt(eq[:], pr[:], bc(m), ALU.is_equal))
                        ch(tt(eq[:], eq[:], w8b, ALU.mult))
                        ch(nc.vector.reduce_max(v[:, 5, :], eq[:], AX))
                        ch(tt(out, eq[:], bc(v[:, 5, :]), ALU.is_equal))

                    pick(m1, s1)
                    ch(nc.vector.scalar_tensor_tensor(out=pr[:], in0=s1, scalar=-2.0, in1=pr[:],
                                                      op0=ALU.mult, op1=ALU.add))
                    pick(v[:, 4, :], s2)
                    ch(tt(M[s.slot(-2, 2)][:], s1, s2, ALU.add), hold=False)
                    ch(tt(DD[:, blk], v[:, 4, :], m1, ALU.subtract), hold=False)
                    assert ch.k == KD
                if s.on(-1, NB):
                    q = s.slot(-1)
                    wait(dve, (s_rs, 3 * s.n()), (s_sc[q], 16 * TOPK * JT * s.lap(-1)), (s_tp, s.n(-3)))
                    for j in range(JT):
                        nc.vector.tensor_scalar(n0[q][:, j, :], flat(XR[:, bass.ds(JT * s.n(-1) + j, 1), :]),
                                                mv[q][:, j, 0:1], rs[q][:, j:j + 1], ALU.subtract, ALU.mult
                                                ).then_inc(s_C, 1)
                if s.on(-2, NB):
                    q = s.slot(-2)
                    ce = Chain(dve, s_E, KE * s.n(-2))
                    rk = psR[:, 0:(JT + 1) * E].rearrange("p (j e) -> p j e", e=E)
                    wait(dve, (s_rk, s.n(-1)), (s_sc[q], 16 * TOPK * JT * s.lap(-2)))
                    ce(tt(po[:], rk[:, 0:JT, :], run[:].unsqueeze(1).broadcast_to([P, JT, E]), ALU.add))
                    ce(tt(run[:], run[:], rk[:, JT, :], ALU.add))
                    for k, (pk, rows) in enumerate(((s1, P1), (s2, P2))):
                        ce(tt(eq[:], po[:], pk, ALU.mult))
                        ce(nc.vector.reduce_sum(v[:, 6 + k, :], eq[:], AX))
                        ce(nc.vector.tensor_copy(idx[q][:, k, :], v[:, 6 + k, :]), hold=False)
                        ce(nc.vector.tensor_copy(rows[:, blk], v[:, 6 + k, :]), hold=False)
                    assert ce.k == KE
                    wait(dve, (s_sg, s.n(-1)), (s_dn, s.n(-3)))
                    tt(h[s.slot(-2, 2)][:], psU[:], sg[s.slot(-2, 2)][:], ALU.mult).then_inc(s_h, 1)
                if s.on(-3, NB):
                    x = XR[:, bass.ds(JT * s.n(-3), JT), :]
                    wait(dve, (s_dn, s.n(-2)))
                    nc.vector.scalar_tensor_tensor(out=x, in0=psY[:], scalar=0.5, in1=x,
                                                   op0=ALU.mult, op1=ALU.add).then_inc(s_add, 1)
                if s.on(-1, NB):
                    wait(dve, (s_hi, s.n()))
                    w = bass.ds(WCH * s.n(-1), WCH)
                    tt(Wl[:, w], Wf[:, w], Wh[:, w].bitcast(F32), ALU.subtract).then_inc(s_lo, 1)
            run_steps(dve, 0, NB + 3, 8, NB, emit)

        @block.scalar
        def _(act):
            act.wait_ge(s_wf, 32)

            def emit(s):
                if s.on(-2, NB):
                    wait(act, (s_D, KD * s.n(-2) + 2))
                    nc.scalar.activation(ez[:], z[:], ACT.Exp).then_inc(s_ex, 1)
                if s.on(-1, NB):
                    w = bass.ds(WCH * s.n(-1), WCH)
                    nc.scalar.activation(Wh[:, w], Wf[:, w], ACT.Copy).then_inc(s_hi, 1)
                    q = s.slot(-1, 2)
                    wait(act, (s_tp, s.n()), (s_gu, s.n(-2)))
                    nc.scalar.activation(nT[q][:], psT[:], ACT.Identity, bias=bet[:], scale=gam[:]).then_inc(s_nT, 1)
                    wait(act, (s_gu, s.n()), (s_h, s.n(-2)))
                    nc.scalar.activation(sg[q][:], psG[:], ACT.Silu).then_inc(s_sg, 1)
            run_steps(act, 0, NB + 2, 4, NB, emit)

        @block.tensor
        def _(pe):
            pe.wait_ge(s_w, 16 * NW)

            def emit(s):
                if s.on(-2, NB):
                    m = M[s.slot(-2, 2)]
                    wait(pe, (s_D, KD * s.n(-1)), (s_E, KE * s.n(-2)))
                    nc.tensor.matmul(psR[:, 0:JT * E], tri[:], flat(m[:]), start=True, stop=False,
                                     skip_group_check=True)
                    for j in range(JT):
                        r = nc.tensor.matmul(psR[:, (j + 1) * E:(JT + 1) * E], ones[:],
                                             m[:, j:j + 1, :].broadcast_to([P, JT - j, E]), start=False,
                                             stop=j == JT - 1, skip_group_check=True)
                    r.then_inc(s_rk, 1)
                if s.on(-1, NB):
                    q4, q = s.slot(-1), s.slot(-1, 2)
                    wait(pe, (s_C, JT * s.n()), (s_nT, s.n(-1)))
                    for j in range(JT):
                        t = nc.tensor.transpose(psT[:, j * P:(j + 1) * P], n0[q4][:, j, :], ident[:])
                    t.then_inc(s_tp, 1)
                    wait(pe, (s_nT, s.n()), (s_D, KD * s.n(-2)))
                    for j in range(JT):
                        t = nc.tensor.matmul(psL[q][:, j * E:(j + 1) * E], nT[q][:, j * P:(j + 1) * P], rT[:],
                                             start=True, stop=True)
                    t.then_inc(s_lg, 1)
                if s.on(-2, NB):
                    q = s.slot(-2, 2)
                    wait(pe, (s_h, s.n(-1)), (s_add, s.n(-2)))
                    for j in range(JT):
                        t = nc.tensor.matmul(psY[:, j, :], h[q][:, j * P:(j + 1) * P], sdT[:], start=True, stop=True)
                    t.then_inc(s_dn, 1)
                if s.on(-1, NB):
                    q = s.slot(-1, 2)
                    wait(pe, (s_sg, s.n(-1)), (s_h, s.n(-1)))
                    nc.tensor.matmul(psG[:], sgT[:], nT[q][:], start=True, stop=True)
                    nc.tensor.matmul(psU[:], suT[:], nT[q][:], start=True, stop=True).then_inc(s_gu, 1)
                if add_attention and s.on(1, NB):
                    oproj(s, 1)

            def oproj(s, off):
                q = s.slot(off)
                wait(pe, (s_os[q], 16 * (s.lap(off) + 1)), (s_oa, s.n(off)))
                nc.tensor.matmul(psE[:], ones[0:1, :], bo[:].unsqueeze(1).broadcast_to([1, JT, D]), start=True,
                                 stop=False, skip_group_check=True)
                for j in range(JT):
                    t = nc.tensor.matmul(psE[:, j, :], Os[q][:, j * P:(j + 1) * P], wo[:], start=False,
                                         stop=j == JT - 1, skip_group_check=True)
                t.then_inc(s_o, 1)

            if add_attention:
                oproj(Step(0, 0), 0)
            run_steps(pe, 0, NB + 2, 4, NB - 4, emit)


def tile_map(K, tag, R):
    nc, T, sb, xd = (K[k] for k in ("nc", "T", "sb", "xd"))
    S1, S2, P1, P2, DD, Y1, Y2, G1, G2, run, tab = (
        R[k] for k in ("S1", "S2", "P1", "P2", "DD", "Y1", "Y2", "G1", "G2", "run", "tab"))
    tag = tag + "m"
    with ExitStack() as c:
        erow = sb(c, tag + "_erow", [P, E])
        part = sb(c, tag + "_part", [P, 1])
        lower = sb(c, tag + "_lower", [P, E, E])
        tau = sb(c, tag + "_tau", [1, ET])
        a = sb(c, tag + "_a", [P, 8, E])
        ti = sb(c, tag + "_ti", [P, 2, E], I32)
        pad = sb(c, tag + "_pad", [P, E], U32)
        zero = sb(c, tag + "_zero", [P, D])
        big = sb(c, tag + "_big", [P, NT, E])
        e2 = sb(c, tag + "_e2", [P, NT])
        sh = sb(c, tag + "_sh", [P, NT])
        m = sb(c, tag + "_m", [P, E, E])
        cm = sb(c, tag + "_cm", [1, ET, E])
        tv = sb(c, tag + "_tv", [1, 6, ET])
        S = Sems(nc, c, tag)
        s_w, s_v, s_p, s_a, s_z = (S(x) for x in ("w", "chain", "pad", "exp", "zero"))
        block = c.enter_context(nc.Block())

        @block.sync
        def _(sp):
            for dst, src in ((erow, "erow"), (part, "part"), (lower, "lower"), (tau, "tau")):
                sp.dma_start(dst[:], T[src]).then_inc(s_w, 16)

        @block.scalar
        def _(act):
            nc.scalar.activation(e2[:], DD[:], ACT.Exp).then_inc(s_a, 1)

        @block.gpsimd
        def _(pool):
            nc.gpsimd.memset(zero[:], 0.0).then_inc(s_z, 1)
            pool.wait_ge(s_z, 1)
            pool.wait_ge(s_v, 2)
            for e in range(E):
                pool.indirect_dma_start(xd, bass.IndirectOffsetOnAxis(pad[:, e:e + 1], 0), zero[:], None
                                        ).then_inc(s_p, 16)
            pool.wait_ge(s_p, 16 * E)

        @block.vector
        def _(dve):
            ch = Chain(dve, s_v, 0)
            tt, ts = nc.vector.tensor_tensor, nc.vector.tensor_scalar
            cnt, tf, incl, excl, dl = (a[:, k, :] for k in range(5))
            dve.wait_ge(s_w, 64)
            ch(ts(a[:, 5, :], run[:], part[:], None, ALU.add))
            ch(nc.vector.tensor_copy(pad[:], a[:, 5, :]))
            ch(tt(cnt, run[:], erow[:], ALU.subtract))
            ch(ts(ti[:, 0, :], cnt, float(P - 1), None, ALU.add))
            ch(ts(ti[:, 1, :], ti[:, 0, :], P.bit_length() - 1, None, ALU.logical_shift_right))
            ch(nc.vector.tensor_copy(tf, ti[:, 1, :]))
            ch(tt(m[:], lower[:], tf.unsqueeze(1).broadcast_to([P, E, E]), ALU.mult))
            ch(nc.vector.reduce_sum(incl, m[:], AX))
            ch(tt(excl, incl, tf, ALU.subtract))
            ch(nc.vector.scalar_tensor_tensor(out=dl, in0=excl, scalar=float(P), in1=erow[:],
                                              op0=ALU.mult, op1=ALU.subtract))
            for pk, rows, out in ((S1, P1, Y1), (S2, P2, Y2)):
                ch(tt(big[:], pk[:], dl.unsqueeze(1).broadcast_to([P, NT, E]), ALU.mult))
                ch(nc.vector.reduce_sum(sh[:], big[:], AX))
                ch(tt(out[:], rows[:], sh[:], ALU.add))
            dve.wait_ge(s_a, 1)
            ch(ts(sh[:], e2[:], 1.0, None, ALU.add))
            ch(nc.vector.reciprocal(G2[:], sh[:]))
            ch(ts(G1[:], G2[:], 0.5, None, ALU.mult))
            ch(tt(G2[:], G1[:], e2[:], ALU.mult))
            ex, nb, ok, t0, t1, t2 = (tv[:, k, :] for k in range(6))
            ch(tt(cm[:], tau[:].unsqueeze(2).broadcast_to([1, ET, E]),
                  incl[0:1, :].unsqueeze(1).broadcast_to([1, ET, E]), ALU.is_ge))
            ch(nc.vector.reduce_sum(ex, cm[:], AX))
            ch(tt(cm[:], cm[:], tf[0:1, :].unsqueeze(1).broadcast_to([1, ET, E]), ALU.mult))
            ch(nc.vector.reduce_sum(nb, cm[:], AX))
            ch(ts(ok, ex, float(E), None, ALU.is_lt))
            ch(tt(t0, ex, ok, ALU.mult))
            ch(nc.vector.tensor_copy(tab[:, 0, :], t0))
            ch(ts(t1, ex, float(REG // P), None, ALU.mult))
            ch(tt(t2, tau[:], nb, ALU.subtract))
            ch(tt(t1, t1, t2, ALU.add))
            ch(tt(t2, t1, ok, ALU.mult))
            ch(nc.vector.tensor_copy(tab[:, 1, :], t2))


def experts(K, tag, R):
    nc, sb, ps, ident, gam, bet, xd, yd = (K[k] for k in ("nc", "sb", "ps", "ident", "gam", "bet", "xd", "yd"))
    tab, Wh, Wl, Wd = (R[k] for k in ("tab", "Wh", "Wl", "Wd"))
    tag = tag + "x"
    with ExitStack() as c:
        Xs = [sb(c, f"{tag}_Xs{q}", [P, D]) for q in range(4)]
        Xf = [sb(c, f"{tag}_Xf{q}", [P, P]) for q in range(2)]
        Xh = [sb(c, f"{tag}_Xh{q}", [P, P], F32R) for q in range(2)]
        Xl = [sb(c, f"{tag}_Xl{q}", [P, P], F32R) for q in range(2)]
        sg = [sb(c, f"{tag}_sg{q}", [P, FF]) for q in range(2)]
        h = [sb(c, f"{tag}_h{q}", [P, FF]) for q in range(2)]
        hT = [sb(c, f"{tag}_hT{q}", [P, FC, P]) for q in range(2)]
        Ys = [sb(c, f"{tag}_Ys{q}", [P, D]) for q in range(4)]
        psX = ps(c, tag + "_psX", [P, P])
        psG = [ps(c, f"{tag}_psG{q}", [P, 512]) for q in range(2)]
        psU = [ps(c, f"{tag}_psU{q}", [P, 512]) for q in range(2)]
        psH = ps(c, tag + "_psH", [P, FC, P])
        psY = [ps(c, f"{tag}_psY{q}", [P, 512]) for q in range(2)]
        S = Sems(nc, c, tag)
        s_ld = [S(f"in{q}") for q in range(4)]
        s_st = [S(f"out{q}") for q in range(4)]
        s_tx, s_xf, s_hl, s_gu, s_sg, s_h, s_th, s_ht, s_dn, s_y = (
            S(x) for x in ("tx", "xf", "hilo", "gateup", "silu", "hidden", "th", "hT", "down", "y"))
        block = c.enter_context(nc.Block())
        LOOP = (4, ET - 4)

        @block.sync
        def _(sp):
            def load(s, off):
                q = s.slot(off)
                row = sp.value_load(tab[0:1, 1, bass.ds(s.n(off), 1)], min_val=0, max_val=E * REG // P - 1)
                wait(sp, (s_tx, s.n(off - 3)))
                sp.dma_start(Xs[q][:], xd[bass.ds(row * P, P), :]).then_inc(s_ld[q], 16)

            for k in range(2):
                load(Step(0, k), 0)

            def emit(s):
                if s.on(2, ET):
                    load(s, 2)
                if s.on(-3, ET):
                    q = s.slot(-3)
                    wait(sp, (s_y, s.n(-2)))
                    sp.dma_start(yd[bass.ds(P * s.n(-3), P), :], Ys[q][:]).then_inc(s_st[q], 16)
            run_steps(sp, 0, ET + 3, *LOOP, emit)
            for q in range(4):
                sp.wait_ge(s_st[q], 16 * (ET // 4))

        @block.tensor
        def _(pe):
            def tx(s, off):
                q = s.slot(off)
                wait(pe, (s_ld[q], 16 * (s.lap(off) + 1)), (s_xf, s.n(off)))
                nc.tensor.transpose(psX[:], Xs[q][:], ident[:]).then_inc(s_tx, 1)

            tx(Step(0, 0), 0)

            def emit(s):
                if s.on(1, ET):
                    tx(s, 1)
                if s.on(0, ET):
                    q = s.slot(0, 2)
                    e = pe.value_load(tab[0:1, 0, bass.ds(s.n(), 1)], min_val=0, max_val=E - 1)
                    wait(pe, (s_hl, 2 * s.n(1)), (s_h, s.n(-1)))
                    for dst, at in ((psG[q], 0), (psU[q], FF)):
                        wh, wl = (w[:, bass.ds(e * (2 * FF) + at, FF)] for w in (Wh, Wl))
                        nc.tensor.matmul(dst[:, 0:FF], Xh[q][:], wh, start=True, stop=False)
                        nc.tensor.matmul(dst[:, 0:FF], Xh[q][:], wl, start=False, stop=False)
                        m = nc.tensor.matmul(dst[:, 0:FF], Xl[q][:], wh, start=False, stop=True)
                        m.then_inc(s_gu, 1)
                if s.on(-1, ET):
                    q = s.slot(-1, 2)
                    wait(pe, (s_h, s.n()), (s_ht, s.n(-1)))
                    for f in range(FC):
                        m = nc.tensor.transpose(psH[:, f, :], h[q][:, f * P:(f + 1) * P], ident[:])
                    m.then_inc(s_th, 1)
                if s.on(-2, ET):
                    q = s.slot(-2, 2)
                    e = pe.value_load(tab[0:1, 0, bass.ds(s.n(-2), 1)], min_val=0, max_val=E - 1)
                    wait(pe, (s_ht, s.n(-1)), (s_y, s.n(-3)))
                    for f in range(FC):
                        w = Wd[:, bass.ds(e * FC + f, 1), :].rearrange("p o n -> p (o n)")
                        m = nc.tensor.matmul(psY[q][:, 0:P], hT[q][:, f, :], w, start=f == 0, stop=f == FC - 1)
                    m.then_inc(s_dn, 1)
            run_steps(pe, 0, ET + 2, *LOOP, emit)

        @block.scalar
        def _(act):
            def xf(s, off):
                wait(act, (s_tx, s.n(off + 1)), (s_hl, 2 * s.n(off - 1)))
                nc.scalar.activation(Xf[s.slot(off, 2)][:], psX[:], ACT.Identity, bias=bet[:], scale=gam[:]
                                     ).then_inc(s_xf, 1)

            xf(Step(0, 0), 0)

            def emit(s):
                if s.on(1, ET):
                    xf(s, 1)
                if s.on(0, ET):
                    q = s.slot(0, 2)
                    wait(act, (s_gu, 2 * s.n() + 1), (s_h, s.n(-1)))
                    nc.scalar.activation(sg[q][:], psG[q][:, 0:FF], ACT.Silu).then_inc(s_sg, 1)
                if s.on(-1, ET):
                    q = s.slot(-1, 2)
                    wait(act, (s_th, s.n()), (s_dn, s.n(-2)))
                    nc.scalar.activation(hT[q][:], psH[:], ACT.Copy).then_inc(s_ht, 1)
            run_steps(act, 0, ET + 1, *LOOP, emit)

        @block.vector
        def _(dve):
            def hilo(s, off):
                q = s.slot(off, 2)
                wait(dve, (s_xf, s.n(off + 1)), (s_gu, 2 * s.n(off - 1)))
                nc.vector.tensor_copy(Xh[q][:], Xf[q][:]).then_inc(s_hl, 1)
                wait(dve, (s_hl, 2 * s.n(off) + 1))
                nc.vector.tensor_tensor(Xl[q][:], Xf[q][:], Xh[q][:].bitcast(F32), ALU.subtract).then_inc(s_hl, 1)

            hilo(Step(0, 0), 0)

            def emit(s):
                if s.on(1, ET):
                    hilo(s, 1)
                if s.on(0, ET):
                    q = s.slot(0, 2)
                    wait(dve, (s_sg, s.n(1)), (s_gu, 2 * s.n(1)), (s_th, s.n(-1)))
                    nc.vector.tensor_tensor(h[q][:], psU[q][:, 0:FF], sg[q][:], ALU.mult).then_inc(s_h, 1)
                if s.on(-2, ET):
                    q4 = s.slot(-2)
                    wait(dve, (s_dn, s.n(-1)), (s_st[q4], 16 * s.lap(-2)))
                    nc.vector.tensor_copy(Ys[q4][:], psY[s.slot(-2, 2)][:, 0:P]).then_inc(s_y, 1)
            run_steps(dve, 0, ET + 2, 8, ET - 4, emit)


def combine(K, tag, R, last):
    nc, T, sb, ps, XR, ident, mhalf, eps, yd, rec, qd = (
        K[k] for k in ("nc", "T", "sb", "ps", "XR", "ident", "mhalf", "eps", "yd", "rec", "qd"))
    Y1, Y2, G1, G2 = (R[k] for k in ("Y1", "Y2", "G1", "G2"))
    tag = tag + "c"
    with ExitStack() as c:
        idx = [sb(c, f"{tag}_idx{q}", [P, TOPK, JT], U32) for q in range(4)]
        Y = [sb(c, f"{tag}_Y{q}", [P, TOPK, JT, D]) for q in range(4)]
        S = Sems(nc, c, tag)
        s_ix, s_cb = S("idx"), S("combined")
        s_ga = [S(f"gathered{q}") for q in range(4)]
        s_st = [S(f"stored{q}") for q in range(4)]
        KC, KA, KR = 2 * JT, 2 * JT, 5
        if not last:
            s_A, s_rs, s_C, s_tp, s_xT, s_mm, s_f, s_r, s_w, s_bk = (
                S(x) for x in ("stats", "rstd", "normed", "transp", "xT", "qkv", "qkvf", "rec", "w", "scaled"))
            wq, wk, wv = (sb(c, f"{tag}_{w}", [P, D]) for w in ("WqT", "WkT", "WvT"))
            bq, bk, bks, bv = (sb(c, f"{tag}_{w}", [P, 1]) for w in ("bq", "bk", "bks", "bv"))
            st = sb(c, tag + "_stats", [P, JT, 6])
            mv = [sb(c, f"{tag}_mv{q}", [P, JT, 2]) for q in range(4)]
            ve = sb(c, tag + "_ve", [P, JT])
            rs = [sb(c, f"{tag}_rs{q}", [P, JT]) for q in range(4)]
            xn = [sb(c, f"{tag}_xn{q}", [P, JT, D]) for q in range(2)]
            xT = sb(c, tag + "_xT", [P, L])
            Qf, Kf, Vf = ([sb(c, f"{tag}_{w}{q}", [P, L]) for q in range(2)] for w in ("Qf", "Kf", "Vf"))
            rc = [sb(c, f"{tag}_rec{q}", [P, REC], F32R) for q in range(4)]
            psT = ps(c, tag + "_psT", [P, L])
            psQ = [ps(c, f"{tag}_psQ{q}", [P, L]) for q in range(3)]
        isq = float(1.0 / np.sqrt(HD))
        block = c.enter_context(nc.Block())

        @block.sync
        def _(sp):
            if not last:
                for dst, src in ((wq, "WqT"), (wk, "WkT"), (wv, "WvT"), (bq, "bq"), (bk, "bk"), (bv, "bv")):
                    sp.dma_start(dst[:], T[src]).then_inc(s_w, 16)

            def emit(s):
                if last and s.on(-1, NB):
                    wait(sp, (s_cb, KC * s.n()))
                    ov = T["out"].rearrange("(n p) d -> p n d", p=P)[:, bass.ds(JT * s.n(-1), JT), :]
                    sp.dma_start(ov, XR[:, bass.ds(JT * s.n(-1), JT), :]).then_inc(s_st[s.slot(-1)], 16)
                if not last and s.on(-3, NB):
                    q, b = s.slot(-3), s.n(-3)
                    wait(sp, (s_r, KR * s.n(-2)))
                    sp.dma_start(rec[bass.ds(b, 1), :, :].rearrange("a p n -> (a p) n"), rc[q][:].bitcast(F32)
                                 ).then_inc(s_st[q], 16)
                    for part in range(2):
                        src = rc[q][:, (2 + part) * L:(3 + part) * L].bitcast(F32).rearrange(
                            "p (a t) -> p a t", a=A8)
                        dst = qd[bass.ds(b, 1), part, :, :, :].rearrange("b a p t -> p (b a) t")
                        sp.dma_start(dst, src).then_inc(s_st[q], 16)
            run_steps(sp, 0, NB + 3, 4, NB, emit)
            for q in range(4):
                sp.wait_ge(s_st[q], 16 * (1 if last else 3) * (NB // 4))

        @block.gpsimd
        def _(pool):
            def rows(s, off):
                blk = bass.ds(JT * s.n(off), JT)
                for k, row in enumerate((Y1, Y2)):
                    nc.gpsimd.tensor_copy(idx[s.slot(off)][:, k, :], row[:, blk]).then_inc(s_ix, 1)

            rows(Step(0, 0), 0)

            def emit(s):
                if s.on(0, NB):
                    wait(pool, (s_ix, 2 * s.n(1)), (s_cb, KC * s.n(-2)))
                if s.on(1, NB):
                    rows(s, 1)
                if not last and s.on(-1, NB):
                    q = s.slot(-1)
                    wait(pool, (s_A, KA * s.n()))
                    nc.gpsimd.tensor_tensor(ve[:], mv[q][:, :, 1], eps[:], ALU.add).then_inc(s_rs, 1)
                    wait(pool, (s_rs, 2 * s.n(-1) + 1), (s_C, JT * s.n(-3)))
                    nc.gpsimd.tensor_tensor(rs[q][:], ve[:], mhalf[:], ALU.pow).then_inc(s_rs, 1)
                if s.on(0, NB):
                    q = s.slot()
                    for k in range(TOPK):
                        for j in range(JT):
                            pool.indirect_dma_start(Y[q][:, k, j, :], None, yd,
                                                    bass.IndirectOffsetOnAxis(idx[q][:, k, j:j + 1], 0)
                                                    ).then_inc(s_ga[q], 16)
            run_steps(pool, 0, NB + 1, 4, NB - 4, emit)

        @block.vector
        def _(dve):
            def emit(s):
                if s.on(-1, NB):
                    q = s.slot(-1)
                    wait(dve, (s_ga[q], 16 * TOPK * JT * (s.lap(-1) + 1)))
                    for k, gate in ((0, G1), (1, G2)):
                        for j in range(JT):
                            t = JT * s.n(-1) + j
                            x = XR[:, bass.ds(t, 1), :].rearrange("p o d -> p (o d)")
                            nc.vector.scalar_tensor_tensor(out=x, in0=Y[q][:, k, j, :], scalar=gate[:, bass.ds(t, 1)],
                                                           in1=x, op0=ALU.mult, op1=ALU.add).then_inc(s_cb, 1)
                        wait(dve, (s_cb, KC * s.n(-1) + JT * (k + 1)))
                if last:
                    return
                if s.on(-1, NB):
                    wait(dve, (s_A, KA * s.n(-1)))
                if s.on(-2, NB):
                    q = s.slot(-2)
                    wait(dve, (s_rs, 2 * s.n(-1)), (s_tp, s.n(-3)))
                    for j in range(JT):
                        nc.vector.tensor_scalar(xn[s.slot(-2, 2)][:, j, :],
                                                flat(XR[:, bass.ds(JT * s.n(-2) + j, 1), :]),
                                                mv[q][:, j, 0:1], rs[q][:, j:j + 1], ALU.subtract, ALU.mult
                                                ).then_inc(s_C, 1)
                if s.on(-1, NB):
                    for j in range(JT):
                        nc.vector.bn_stats(st[:, j, :], flat(XR[:, bass.ds(JT * s.n(-1) + j, 1), :])).then_inc(s_A, 1)
                    wait(dve, (s_A, KA * s.n(-1) + JT))
                if s.on(-3, NB):
                    q, q2 = s.slot(-3), s.slot(-3, 2)
                    r = rc[q]
                    base = KR * s.n(-3)
                    wait(dve, (s_f, 3 * s.n(-2)), (s_st[q], 48 * s.lap(-3)))
                    nc.vector.tensor_copy(r[:, 2 * L:3 * L], Qf[q2][:]).then_inc(s_r, 1)
                    nc.vector.tensor_copy(r[:, 0:L], Kf[q2][:]).then_inc(s_r, 1)
                    wait(dve, (s_r, base + 2))
                    nc.vector.tensor_tensor(r[:, 3 * L:4 * L], Qf[q2][:], r[:, 2 * L:3 * L].bitcast(F32), ALU.subtract
                                            ).then_inc(s_r, 1)
                    nc.vector.tensor_tensor(r[:, L:2 * L], Kf[q2][:], r[:, 0:L].bitcast(F32), ALU.subtract
                                            ).then_inc(s_r, 1)
                    nc.vector.transpose(r[:, 4 * L:5 * L].bitcast(F32), Vf[q2][:]).then_inc(s_r, 1)
                if s.on(-1, NB):
                    for j in range(JT):
                        nc.vector.bn_aggr(mv[s.slot(-1)][:, j, :], st[:, j, :]).then_inc(s_A, 1)
            run_steps(dve, 0, NB + 3, 8, NB, emit)

        if last:
            return

        @block.scalar
        def _(act):
            act.wait_ge(s_w, 96)
            nc.scalar.activation(bks[:], bk[:], ACT.Copy, scale=isq).then_inc(s_bk, 1)
            act.wait_ge(s_bk, 1)

            def emit(s):
                if s.on(-2, NB):
                    q2 = s.slot(-2, 2)
                    wait(act, (s_tp, s.n(-1)), (s_mm, 3 * s.n(-2)))
                    nc.scalar.activation(xT[:], psT[:], ACT.Copy).then_inc(s_xT, 1)
                    wait(act, (s_r, KR * s.n(-3)))
                    for n, (dst, bias, scale) in enumerate(((Qf, bq, 1.0), (Kf, bks, isq), (Vf, bv, 1.0))):
                        wait(act, (s_mm, 3 * s.n(-2) + n + 1))
                        nc.scalar.activation(dst[q2][:], psQ[n][:], ACT.Identity, bias=bias[:], scale=scale
                                             ).then_inc(s_f, 1)
            run_steps(act, 0, NB + 2, 4, NB, emit)

        @block.tensor
        def _(pe):
            pe.wait_ge(s_w, 96)

            def emit(s):
                if s.on(-2, NB):
                    wait(pe, (s_C, JT * s.n(-1)), (s_xT, s.n(-2)))
                    for j in range(JT):
                        m = nc.tensor.transpose(psT[:, j * P:(j + 1) * P], xn[s.slot(-2, 2)][:, j, :], ident[:])
                    m.then_inc(s_tp, 1)
                    wait(pe, (s_xT, s.n(-1)), (s_f, 3 * s.n(-2)))
                    for n, w in enumerate((wq, wk, wv)):
                        nc.tensor.matmul(psQ[n][:], w[:], xT[:], start=True, stop=True).then_inc(s_mm, 1)
            run_steps(pe, 0, NB + 2, 4, NB, emit)


def attention(K):
    nc, T, sb, ps, rec, qd, rsd, otd = (K[k] for k in ("nc", "T", "sb", "ps", "rec", "qd", "rsd", "otd"))
    with ExitStack() as c:
        RA = sb(c, "rel_hi", [P, RELW], F32R)
        RB = sb(c, "rel_lo", [P, RELW], F32R)
        RF = sb(c, "rel_f32", [P, RELW])
        maskh = sb(c, "mask_head", [P, H])
        maska = sb(c, "mask_a", [P, A8])
        KQ = sb(c, "record_ring", [P, 2, REC], F32R)
        M0 = sb(c, "q_by_query_ring", [P, 2, H, NQ])
        NS = 8
        SQ = [sb(c, f"stat_q{s}", [P, 2, H, A8], F32R) for s in range(NS)]
        SR = [sb(c, f"stat_r{s}", [P, H, A8], F32R) for s in range(NS)]
        nmx = sb(c, "neg_max", [P, 4])
        Pr = [sb(c, f"probs{s}", [P, L]) for s in range(4)]
        PT = [sb(c, f"probs_T{s}", [P, KEYS32, 4, GT, A8]) for s in range(2)]
        W = sb(c, "values_diag", [P, 4, KEYS32, 4, HD])
        rs = sb(c, "row_sum", [P, 2, GT])
        rb = sb(c, "row_sum_T", [P, 2, A8, GT])
        ri = sb(c, "recip_sum", [P, A8, GT])
        OT = sb(c, "attn_out", [P, A8, NQ])
        psS = [ps(c, f"ps_scores{s}", [P, L]) for s in range(4)]
        psO = [ps(c, f"ps_out{s}", [P, GT, A8]) for s in range(2)]
        S = Sems(nc, c, "att")
        (s_rf, s_rh, s_rec, s_m0, s_ex, s_sc, s_mx, s_p, s_tr, s_wz, s_we, s_pv, s_rs, s_rb, s_ri, s_o, s_ot, s_mk) = (
            S(x) for x in ("relf", "rel", "rec", "m0", "expanded", "scores", "max", "probs", "transposed", "wzero",
                           "wexp", "pv", "rsum_out", "rsum_in", "recip", "out", "out_st", "masks"))
        block = c.enter_context(nc.Block())

        @block.sync
        def _(sp):
            for part in range(2):
                for a in range(A8):
                    p0 = part * 64 + a * HD
                    off = L - 1 - (NQ - 1) - NQ * a
                    sp.dma_start(RF[p0:p0 + HD, :], T["relT"][:, off:off + RELW]).then_inc(s_rf, 16)
            sp.dma_start(maskh[:], T["maskh"]).then_inc(s_mk, 16)
            sp.dma_start(maska[:], T["maska"]).then_inc(s_mk, 16)

            def load(b, par):
                sp.dma_start(KQ[:, bass.ds(par, 1), :].rearrange("p o n -> p (o n)").bitcast(F32),
                             rec[bass.ds(b, 1), :, :].rearrange("a p n -> (a p) n")).then_inc(s_rec, 16)
                for part in range(2):
                    for a in range(A8):
                        p0 = part * 64 + a * HD
                        src = qd[bass.ds(b, 1), part, a, :, :].rearrange("b (h d) t -> d (b h) t", d=HD)
                        sp.dma_start(M0[p0:p0 + HD, bass.ds(par, 1), :, :].rearrange("p o h t -> p (o h) t"), src
                                     ).then_inc(s_m0, 16)

            def seq(b, first, last):
                wait(sp, (s_rec, 16 * (b + 1)), (s_m0, 256 * (b + 1)))
                for g in range(NG):
                    G = b * NG + g
                    wait(sp, (s_p, (G + 1) * GT))
                    sp.dma_start(rsd[bass.ds(G, 1), :, :].rearrange("o p t -> (o p) t"), rs[:, g % 2, :]
                                 ).then_inc(s_rs, 16)
                    wait(sp, (s_rs, 16 * (G + 1)), (s_ri, G - 1), (s_rb, 64 * G))
                    for hh in range(4):
                        src = rsd[bass.ds(G, 1), :, :].rearrange("o (k hh a) t -> hh (o k) (a t)", k=4, hh=4)[hh]
                        src = src.unsqueeze(1).broadcast_to([4, HD, A8 * GT])
                        dst = rb[32 * hh:32 * hh + 32, g % 2, :, :].rearrange("p a t -> p (a t)")
                        sp.dma_start(dst, src).then_inc(s_rb, 16)
                    if g == 0 and not first:
                        wait(sp, (s_o, b * NG))
                        sp.dma_start(otd[bass.ds(b - 1, 1), :, :].rearrange("a p n -> (a p) n"),
                                     OT[:].rearrange("p a t -> p (a t)")).then_inc(s_ot, 16)
                    if g == 1 and not last:
                        wait(sp, (s_sc, b * NQ), (s_we, 4 * b))
                        load(b + 1, (b + 1) % 2)

            load(0, 0)
            seq(0, True, False)
            with sp.Fori(1, B - 1) as b:
                seq(b, False, False)
            seq(B - 1, False, True)
            sp.wait_ge(s_o, B * NG)
            sp.dma_start(otd[B - 1], OT[:].rearrange("p a t -> p (a t)")).then_inc(s_ot, 16)
            sp.wait_ge(s_ot, 16 * B)

        @block.gpsimd
        def _(pool):
            pool.wait_ge(s_mk, 32)
            mh = maskh[:].unsqueeze(2).broadcast_to([P, H, A8]).unsqueeze(1).broadcast_to([P, 2, H, A8])
            ma = maska[:].unsqueeze(1).broadcast_to([P, H, A8])

            def seq(b, first):
                pool.wait_ge(s_rec, 16 * (b + 1))
                pool.wait_ge(s_m0, 256 * (b + 1))
                par = b % 2
                for t in range(NQ):
                    n = b * NQ + t
                    s = t % NS
                    if not (first and t < NS):
                        pool.wait_ge(s_sc, n - NS + 1)
                    q = KQ[:, bass.ds(par, 1), 2 * L:4 * L].bitcast(F32).rearrange(
                        "p o (c a t) -> p (o c) a t", c=2, a=A8)[:, :, :, t]
                    q = q.unsqueeze(2).broadcast_to([P, 2, H, A8])
                    nc.gpsimd.tensor_tensor(SQ[s][:], q, mh, ALU.mult).then_inc(s_ex, 1)
                    m0 = M0[:, bass.ds(par, 1), :, t].rearrange("p o h -> p (o h)")
                    nc.gpsimd.tensor_tensor(SR[s][:], m0.unsqueeze(2).broadcast_to([P, H, A8]), ma, ALU.mult
                                            ).then_inc(s_ex, 1)

            seq(0, True)
            with pool.Fori(1, B) as b:
                seq(b, False)

        @block.tensor
        def _(pe):
            pe.wait_ge(s_rh, 2)

            def values(G, par, first2):
                pe.wait_ge(s_tr, (G + 1) * GT)
                if not first2:
                    pe.wait_ge(s_o, G - 1)
                for r in range(KEYS32):
                    for hh in range(4):
                        m = nc.tensor.matmul(psO[par][32 * hh:32 * hh + 32, :, :].rearrange("p t a -> p (t a)"),
                                             W[:, hh, r, :, :].rearrange("p k d -> p (k d)"),
                                             PT[par][:, r, hh, :, :].rearrange("p t a -> p (t a)"),
                                             start=(r == 0), stop=(r == KEYS32 - 1))
                m.then_inc(s_pv, 1)

            def seq(b, first):
                pe.wait_ge(s_rec, 16 * (b + 1))
                par = b % 2
                for t in range(NQ):
                    n = b * NQ + t
                    s, bank = t % NS, t % 4
                    pe.wait_ge(s_ex, 2 * (n + 1))
                    if not (first and t < 4):
                        pe.wait_ge(s_p, n - 3)
                    khi = KQ[:, bass.ds(par, 1), 0:L].rearrange("p o n -> p (o n)")
                    klo = KQ[:, bass.ds(par, 1), L:2 * L].rearrange("p o n -> p (o n)")
                    qh = SQ[s][:, 0, :, :].rearrange("p h a -> p (h a)")
                    ql = SQ[s][:, 1, :, :].rearrange("p h a -> p (h a)")
                    qr = SR[s][:].rearrange("p h a -> p (h a)")
                    w0 = NQ - 1 - t
                    nc.tensor.matmul(psS[bank][:], qr, RA[:, w0:w0 + L], start=True, stop=False)
                    nc.tensor.matmul(psS[bank][:], qr, RB[:, w0:w0 + L], start=False, stop=False)
                    nc.tensor.matmul(psS[bank][:], qh, khi, start=False, stop=False)
                    nc.tensor.matmul(psS[bank][:], qh, klo, start=False, stop=False)
                    nc.tensor.matmul(psS[bank][:], ql, khi, start=False, stop=True).then_inc(s_sc, 1)
                    if t % GT == 3 and not (first and t == 3):
                        g = t // GT
                        if g == 1:
                            pe.wait_ge(s_we, 4 * (b + 1))
                        values(b * NG + g - 1, (g - 1) % 2, first and g < 3)

            seq(0, True)
            with pe.Fori(1, B) as b:
                seq(b, False)
            values(B * NG - 1, 1, False)

        @block.vector
        def _(dve):
            nc.vector.memset(W[:], 0.0).then_inc(s_wz, 1)
            dve.wait_ge(s_rf, 256)
            nc.vector.tensor_copy(RA[:], RF[:]).then_inc(s_rh, 1)
            dve.wait_ge(s_rh, 1)
            nc.vector.tensor_tensor(RB[:], RF[:], RA[:].bitcast(F32), ALU.subtract).then_inc(s_rh, 1)

            def transpose(b, t, first):
                dve.wait_ge(s_p, b * NQ + t + 1)
                g, tt = t // GT, t % GT
                if tt == 0 and not (first and g < 2):
                    dve.wait_ge(s_pv, b * NG + g - 1)
                nc.vector.transpose(PT[g % 2][:, :, :, tt, :],
                                    Pr[t % 4][:].rearrange("p (r x) -> p r x", x=32)).then_inc(s_tr, 1)

            def norm(G, g, first2, b):
                dve.wait_ge(s_rb, 64 * (G + 1))
                if not (first2 and g == 0):
                    dve.wait_ge(s_o, G)
                nc.vector.reciprocal(ri[:], rb[:, g % 2, :, :]).then_inc(s_ri, 1)
                dve.wait_ge(s_ri, G + 1)
                dve.wait_ge(s_pv, G + 1)
                if g == 0 and not first2:
                    dve.wait_ge(s_ot, 16 * b)
                nc.vector.tensor_tensor(OT[:, :, g * GT:(g + 1) * GT].rearrange("p a t -> p t a"), psO[g % 2][:],
                                        ri[:].rearrange("p a t -> p t a"), ALU.mult).then_inc(s_o, 1)

            def seq(b, first):
                for t in range(NQ):
                    n = b * NQ + t
                    dve.wait_ge(s_sc, n + 1)
                    if not (first and t < 4):
                        dve.wait_ge(s_p, n - 3)
                    nc.vector.reduce_max(nmx[:, t % 4:t % 4 + 1], psS[t % 4][:], AX, negate=True).then_inc(s_mx, 1)
                    if t >= 1:
                        transpose(b, t - 1, first)
                    elif not first:
                        transpose(b - 1, NQ - 1, False)
                    if t % GT == 8 and not (first and t == 8):
                        g = t // GT
                        if g == 0:
                            norm(b * NG - 1, 3, False, b - 1)
                        else:
                            norm(b * NG + g - 1, g - 1, first, b)

            seq(0, True)
            with dve.Fori(1, B) as b:
                seq(b, False)
            transpose(B - 1, NQ - 1, False)
            norm(B * NG - 1, 3, False, B - 1)

        @block.scalar
        def _(act):
            def seq(b, first):
                for t in range(NQ):
                    n = b * NQ + t
                    g, tt = t // GT, t % GT
                    act.wait_ge(s_mx, n + 1)
                    if not (first and t < 4):
                        act.wait_ge(s_tr, n - 3)
                    if tt == 0 and not (first and g < 2):
                        act.wait_ge(s_rs, 16 * (b * NG + g - 1))
                    nc.scalar.activation(Pr[t % 4][:], psS[t % 4][:], ACT.Exp, bias=nmx[:, t % 4:t % 4 + 1],
                                         accum_out=rs[:, g % 2, tt:tt + 1]).then_inc(s_p, 1)
                    if t == 10:
                        if first:
                            act.wait_ge(s_wz, 1)
                        else:
                            act.wait_ge(s_pv, b * NG)
                        act.wait_ge(s_rec, 16 * (b + 1))
                        for k in range(4):
                            p = slice(32 * k, 32 * k + 32)
                            src = KQ[p, bass.ds(b % 2, 1), 4 * L:5 * L].bitcast(F32).rearrange(
                                "p o (r hh d) -> p (o hh) r d", hh=4, d=HD)
                            nc.scalar.activation(W[p, :, :, k, :], src, ACT.Copy).then_inc(s_we, 1)

            seq(0, True)
            with act.Fori(1, B) as b:
                seq(b, False)

_F = np.float32


def kernel(**inputs):
    import concourse.bacc as _bacc
    from concourse.bass_utils import run_bass_kernel_spmd as _run

    a = {k[3:]: np.asarray(v) for k, v in inputs.items()}
    gu, dn = a["ffn_gate_up_w"], a["ffn_down_w"]
    sgu, sdn = a["ffn_shared_gate_up_w"], a["ffn_shared_down_w"]

    rel = a["attn_rel_emb"]
    rel = np.concatenate([rel[MAXLEN - 1:], rel, np.repeat(rel[-1:], L - 1 - (MAXLEN - 1), axis=0)])
    arrays = {
        "x": a["attn_x"].reshape(TOK, D),
        "ident": np.eye(P, dtype=_F),
        "w8": np.broadcast_to(np.arange(E, 0, -1, dtype=_F), (P, E)),
        "maskh": np.kron(np.eye(H, dtype=_F), np.ones((HD, 1), _F)),
        "maska": np.concatenate([np.kron(np.eye(A8, dtype=_F), np.ones((HD, 1), _F))] * 2),
        "gamma": a["ffn_ln_gamma"].reshape(D, 1),
        "beta": a["ffn_ln_beta"].reshape(D, 1),
        "routerT": a["ffn_router_w"].T,
        "erow": np.broadcast_to(np.arange(E, dtype=_F) * _F(REG), (P, E)),
        "tri": np.triu(np.ones((P, P), _F), 1),
        "ones": np.ones((P, P), _F),
        "part": np.arange(P, dtype=_F).reshape(P, 1),
        "lower": np.broadcast_to(np.tril(np.ones((E, E), _F)), (P, E, E)),
        "tau": np.arange(ET, dtype=_F).reshape(1, ET),
        "shG": sgu[:SFF].T, "shU": sgu[SFF:].T, "shD": sdn.T,
        "WguT": gu.reshape(E * 2 * FF, D).T,
        "WdT": dn.transpose(0, 2, 1).reshape(E * FC, P, D).transpose(1, 0, 2),
        "WqT": a["attn_Wq"].T, "WkT": a["attn_Wk"].T, "WvT": a["attn_Wv"].T,
        "bq": a["attn_bq"].reshape(D, 1), "bk": a["attn_bk"].reshape(D, 1), "bv": a["attn_bv"].reshape(D, 1),
        "WoT": a["attn_Wo"].T.reshape(4, 4, HD, D).transpose(1, 0, 2, 3).reshape(D, D),
        "bo": a["attn_bo"].reshape(1, D),
        "relT": rel.T,
    }
    arrays = {f"in_{k}": np.ascontiguousarray(v) for k, v in arrays.items()}
    nc = _bacc.Bacc("TRN2", target_bir_lowering=False, num_devices=1)
    T = {k[3:]: nc.dram_tensor(k, v.shape, F32, kind="ExternalInput").ap() for k, v in arrays.items()}
    T["out"] = nc.dram_tensor("out", (TOK, D), F32, kind="ExternalOutput").ap()
    build(nc, T)
    r = _run(nc, [arrays], core_ids=[0])
    return r.results[0]["out"].reshape(B, L, D)
```

```python
from contextlib import ExitStack

import numpy as np

import concourse.bass as bass
from concourse import mybir

F32 = mybir.dt.float32
F32R = mybir.dt.float32r
BF16 = mybir.dt.bfloat16
I32 = mybir.dt.int32
U32 = mybir.dt.uint32
ALU = mybir.AluOpType
ACT = mybir.ActivationFunctionType
AX = mybir.AxisListType.X

P = 128
D = 128
B, L = 16, 512
TOK = B * L
NT = TOK // P
JT = L // P
NB = NT // JT
E, FF, SFF = 8, 384, 128
TOPK = 2
FC = FF // P
TR = 2 * P
REG = TOK + TR
ET = (TOPK * TOK) // TR + E
DX = D + 1
NPAD = (TR // P) * E
SPARE = NPAD + (TR // P) * (ET - (TOPK * TOK) // TR)
JP = 2 * JT
H, HD = 16, 8
MAXLEN = 256
LN_EPS = 1e-5
A8 = 8
NQ = L // A8
GT = 16
NG = NQ // GT
RELW = L + NQ - 1
KEYS32 = L // 32
VT0 = 3
VEACH = -(-4 * KEYS32 // (GT - VT0))
REC = 2 * L + 2 * L + L


class Sems:

    def __init__(self, nc, ctx, prefix):
        self.nc, self.ctx, self.prefix, self.made = nc, ctx, prefix, {}

    def __call__(self, name):
        if name not in self.made:
            self.made[name] = self.ctx.enter_context(self.nc.semaphore(f"{self.prefix}_{name}"))
        return self.made[name]


def wait(eng, *pairs):
    pairs = [(s, v) for s, v in pairs if not (isinstance(v, int) and v <= 0)]
    for _, v in pairs:
        if not isinstance(v, int):
            eng.compute_val(v)
    for s, v in pairs:
        eng.wait_ge(s, v)


class Step:

    def __init__(self, lap, r):
        self.i, self.r = lap, r

    def n(self, off=0):
        return self.i * 4 + (self.r + off)

    def slot(self, off=0, ring=4):
        return (self.r + off) % ring

    def lap(self, off=0):
        return self.i + (self.r + off) // 4

    def pairs(self, off):
        return self.i * 2 + ((self.r + off) // 2 + 1)

    def pair(self, off):
        return (self.r + off) // 2 % 2

    def on(self, off, count):
        return not isinstance(self.i, int) or 0 <= self.n(off) < count


def run_steps(eng, first, last, loop_from, loop_to, emit):
    for s in range(first, loop_from):
        emit(Step(s // 4, s % 4))
    with eng.Fori(loop_from // 4, loop_to // 4) as i:
        for r in range(4):
            emit(Step(i, r))
    for s in range(loop_to, last):
        emit(Step(s // 4, s % 4))


class Chain:

    def __init__(self, eng, sem, base):
        self.eng, self.sem, self.base, self.k = eng, sem, base, 0

    def __call__(self, ins, hold=True):
        ins.then_inc(self.sem, 1)
        self.k += 1
        if hold:
            wait(self.eng, (self.sem, self.base + self.k))


def flat(ap):
    return ap.rearrange("p a b -> p (a b)")


def build(nc, T):
    with ExitStack() as top:
        def sb(ctx, name, shape, dt=F32):
            return ctx.enter_context(nc.sbuf_tensor(name, shape, dt))

        def ps(ctx, name, shape):
            return ctx.enter_context(nc.psum_tensor(name, shape, F32))

        def dram(name, shape):
            return nc.dram_tensor(name, shape, F32).ap()

        XR = sb(top, "residual", [P, NT, D])
        ident = sb(top, "ident", [P, P])
        mhalf = sb(top, "minus_half", [P, JT])
        eps = sb(top, "eps", [P, JT])
        k1e = sb(top, "one_plus_eps", [P, JT])
        ke2 = sb(top, "eps_squared", [P, JT])
        gam = sb(top, "gamma_col", [P, 1])
        bet = sb(top, "beta_col", [P, 1])

        xd = dram("dispatched", [E * REG + (SPARE - NPAD) * P, DX])
        yd = dram("expert_out", [(TOPK * NT + SPARE) * P, D])
        rec = dram("qkv_record", [B, P, REC])
        rsd = dram("row_sums", [B * NG, P, GT])
        otd = dram("attn_out_T", [B, P, L])
        K = dict(nc=nc, T=T, sb=sb, ps=ps, XR=XR, ident=ident, mhalf=mhalf, eps=eps, k1e=k1e, ke2=ke2, gam=gam, bet=bet, xd=xd, yd=yd,
                 rec=rec, rsd=rsd, otd=otd)

        with nc.semaphore("load_in") as s_in, nc.semaphore("load_c") as s_c, nc.Block() as block:
            @block.sync
            def _(sp):
                xv = T["x"].rearrange("(n p) d -> p n d", p=P)
                for q in range(4):
                    sp.dma_start(XR[:, 16 * q:16 * q + 16, :], xv[:, 16 * q:16 * q + 16, :]).then_inc(s_in, 16)
                sp.wait_ge(s_in, 64)

            @block.scalar
            def _(act):
                act.dma_start(ident[:], T["ident"]).then_inc(s_c, 16)
                act.dma_start(gam[:], T["gamma"]).then_inc(s_c, 16)
                act.dma_start(bet[:], T["beta"]).then_inc(s_c, 16)
                act.wait_ge(s_c, 48)

            @block.vector
            def _(dve):
                for dst, value in ((mhalf, -0.5), (eps, LN_EPS), (k1e, 1.0 + LN_EPS), (ke2, LN_EPS * LN_EPS)):
                    nc.vector.memset(dst[:], value)

        ffn(K, "f1", False)
        attention(K)
        ffn(K, "f2", True)


def ffn(K, tag, last):
    nc, sb = K["nc"], K["sb"]
    with ExitStack() as c:
        R = dict(
            DD=sb(c, tag + "_pdiff", [P, NT]),
            G1=sb(c, tag + "_gate1", [P, NT]),
            G2=sb(c, tag + "_gate2", [P, NT]),
            run=sb(c, tag + "_fill", [P, E]),
            tab=sb(c, tag + "_tiletab", [1, 2, ET], I32),
            Wh=sb(c, tag + "_Wgu_hi", [P, E * 2 * FF], F32R),
            Wl=sb(c, tag + "_Wgu_lo", [P, E * 2 * FF], F32R),
            Wd=sb(c, tag + "_Wd", [P, E * FC, P]),
        )
        dispatch(K, tag, R, last)
        tile_map(K, tag, R)
        experts(K, tag, R)
        combine(K, tag, R, last)


def dispatch(K, tag, R, add_attention):
    nc, T, sb, ps, XR, ident, gam, bet, mhalf, k1e, ke2, xd = (
        K[k] for k in ("nc", "T", "sb", "ps", "XR", "ident", "gam", "bet", "mhalf", "k1e", "ke2", "xd"))
    DD, run, Wh, Wl, Wd = (R[k] for k in ("DD", "run", "Wh", "Wl", "Wd"))
    tag = tag + "d"
    WCH = E * 2 * FF // NB
    with ExitStack() as c:
        Wf = sb(c, tag + "_Wgu", [P, E * 2 * FF])
        rT = sb(c, tag + "_routerT", [P, E])
        w8 = sb(c, tag + "_w8", [P, E])
        erow = sb(c, tag + "_erow", [P, E])
        tri = sb(c, tag + "_tri", [P, P])
        ones = sb(c, tag + "_ones", [P, P])
        sgT = sb(c, tag + "_shG", [P, SFF])
        suT = sb(c, tag + "_shU", [P, SFF])
        sdT = sb(c, tag + "_shD", [P, D])
        st = sb(c, tag + "_stats", [P, JT, 6])
        mv = [sb(c, f"{tag}_mv{q}", [P, JT, 2]) for q in range(4)]
        ve = sb(c, tag + "_ve", [P, JT])
        vf = sb(c, tag + "_vf", [P, JT])
        rs = [sb(c, f"{tag}_rs{q}", [P, JT]) for q in range(4)]
        tid = sb(c, tag + "_tid", [P, TOPK, NT], U32)
        n0 = [[sb(c, f"{tag}_n0{k}{q}", [P, JT, DX]) for q in range(4)] for k in range(TOPK)]
        nT = [sb(c, f"{tag}_nT{q}", [P, L]) for q in range(2)]
        z, ez, pr, eq, s1, s2, po = (sb(c, f"{tag}_{x}", [P, JP, E]) for x in ("z", "ez", "pr", "eq", "s1", "s2", "po"))
        M = [sb(c, f"{tag}_M{q}", [P, JP, E], BF16) for q in range(2)]
        trib = sb(c, tag + "_trib", [P, P], BF16)
        onesb = sb(c, tag + "_onesb", [P, P], BF16)
        v = sb(c, tag + "_v", [P, 8, JP])
        idx = [sb(c, f"{tag}_idx{q}", [P, TOPK, JP], U32) for q in range(2)]
        sg = [sb(c, f"{tag}_sg{q}", [P, L]) for q in range(2)]
        h = [sb(c, f"{tag}_h{q}", [P, L]) for q in range(2)]
        psT = ps(c, tag + "_psT", [P, L])
        psL = [ps(c, f"{tag}_psL{q}", [P, L]) for q in range(2)]
        psR = ps(c, tag + "_psR", [P, L])
        psG = ps(c, tag + "_psG", [P, L])
        psU = ps(c, tag + "_psU", [P, L])
        psY = ps(c, tag + "_psY", [P, JT, D])
        if add_attention:
            psE = ps(c, tag + "_psE", [P, JT, D])
            wo = sb(c, tag + "_WoT", [P, D])
            bo = sb(c, tag + "_bo", [1, D])
            Os = [sb(c, f"{tag}_Os{q}", [P, L]) for q in range(4)]
        S = Sems(nc, c, tag)
        s_w, s_wf, s_A, s_rs, s_C, s_tp, s_nT, s_lg, s_D, s_ex, s_rk, s_E, s_gu, s_sg, s_h, s_dn, s_add, s_hi, s_lo = (
            S(x) for x in ("w", "wf", "stats", "rstd", "normed", "transp", "nT", "logits", "route", "exp", "rank",
                           "rows", "gateup", "silu", "hidden", "down", "added", "whi", "wlo"))
        s_nb, s_bf, s_id = S("copied"), S("bf16"), S("dest")
        s_sc = [S(f"scattered{q}") for q in range(4)]
        if add_attention:
            s_os = [S(f"attn_in{q}") for q in range(4)]
            s_o, s_oa = S("oproj"), S("oadded")
        KA, KC, KD, KE = 8, JT, 18, 8
        NW = 10 + 2 * add_attention
        block = c.enter_context(nc.Block())

        @block.sync
        def _(sp):
            for dst, src in ((rT, "routerT"), (w8, "w8"), (erow, "erow"), (tri, "tri"), (ones, "ones"),
                             (sgT, "shG"), (suT, "shU"), (sdT, "shD")):
                sp.dma_start(dst[:], T[src]).then_inc(s_w, 16)
            sp.dma_start(run[:], T["erow"]).then_inc(s_w, 16)
            sp.dma_start(tid[:], T["tid"]).then_inc(s_w, 16)
            if add_attention:
                sp.dma_start(wo[:], T["WoT"]).then_inc(s_w, 16)
                sp.dma_start(bo[:], T["bo"]).then_inc(s_w, 16)
            sp.dma_start(Wf[:], T["WguT"]).then_inc(s_wf, 16)
            sp.dma_start(Wd[:], T["WdT"]).then_inc(s_wf, 16)
            if add_attention:
                def emit(st_):
                    if st_.on(0, NB):
                        wait(sp, (s_o, st_.n(-3)))
                        sp.dma_start(Os[st_.slot()][:], K["otd"][bass.ds(st_.n(), 1), :, :].rearrange(
                            "a p n -> (a p) n")).then_inc(s_os[st_.slot()], 16)
                run_steps(sp, 0, NB, 4, NB, emit)
            sp.wait_ge(s_wf, 32)

        @block.gpsimd
        def _(pool):
            tt = nc.gpsimd.tensor_tensor
            pool.wait_ge(s_w, 16 * NW)

            def emit(s):
                if s.on(0, NB):
                    wait(pool, (s_A, KA * s.n(1)))
                    tt(ve[:], mv[s.slot()][:, :, 1], k1e[:], ALU.mult).then_inc(s_rs, 1)
                    wait(pool, (s_rs, 3 * s.n() + 1))
                    tt(vf[:], ve[:], ke2[:], ALU.add).then_inc(s_rs, 1)
                    wait(pool, (s_rs, 3 * s.n() + 2), (s_C, KC * s.n(-3)))
                    tt(rs[s.slot()][:], vf[:], mhalf[:], ALU.pow).then_inc(s_rs, 1)
                if s.on(-3, NB):
                    wait(pool, (s_nb, s.n(-2)), (s_id, TOPK * s.n(-2)), (s_E, KE * s.pairs(-3)))
                if s.on(-2, NB):
                    wait(pool, (s_C, KC * s.n(-1)))
                    for k in range(TOPK):
                        nc.gpsimd.tensor_copy(n0[k][s.slot(-2)][:, :, D].bitcast(U32),
                                              tid[:, k, bass.ds(JT * s.n(-2), JT)]).then_inc(s_id, 1)
                if s.on(-3, NB):
                    q = s.slot(-3)
                    for j in range(JT):
                        for k in range(TOPK):
                            at = s.slot(-3, 2) * JT + j
                            pool.indirect_dma_start(
                                xd, bass.IndirectOffsetOnAxis(idx[s.pair(-3)][:, k, at:at + 1], 0),
                                n0[k][q][:, j, :], None).then_inc(s_sc[q], 16)
            run_steps(pool, 0, NB + 3, 4, NB, emit)
            for q in range(4):
                pool.wait_ge(s_sc[q], 16 * TOPK * JT * (NB // 4))

        @block.vector
        def _(dve):
            dve.wait_ge(s_w, 16 * NW)
            tt = nc.vector.tensor_tensor
            nc.vector.tensor_copy(trib[:], tri[:]).then_inc(s_bf, 1)
            nc.vector.tensor_copy(onesb[:], ones[:]).then_inc(s_bf, 1)

            def bc(col):
                return col.unsqueeze(2).broadcast_to([P, JP, E])

            w8b = w8[:].unsqueeze(1).broadcast_to([P, JP, E])

            def emit(s):
                route = s.r % 2 == 1 and s.on(-3, NB)
                if add_attention and s.on(0, NB):
                    x = XR[:, bass.ds(JT * s.n(), JT), :]
                    wait(dve, (s_o, s.n(1)))
                    tt(x, x, psE[:], ALU.add).then_inc(s_oa, 1)
                    wait(dve, (s_oa, s.n(1)))
                if route:
                    ch = Chain(dve, s_D, KD * (s.pairs(-3) - 1))
                    lg = psL[s.pair(-3)][:, 0:JP * E].rearrange("p (j e) -> p j e", e=E)
                    wait(dve, (s_lg, s.n(-1)))
                    ch(nc.vector.reduce_max(v[:, 0, :], lg, AX))
                    ch(tt(z[:], lg, bc(v[:, 0, :]), ALU.subtract), hold=False)
                if s.on(0, NB):
                    wait(dve, (s_A, KA * s.n()))
                if s.on(-1, NB):
                    q = s.slot(-1)
                    wait(dve, (s_rs, 3 * s.n()), (s_sc[q], 16 * TOPK * JT * s.lap(-1)), (s_tp, s.n(-3)))
                    for j in range(JT):
                        nc.vector.tensor_scalar(n0[0][q][:, j, 0:D], flat(XR[:, bass.ds(JT * s.n(-1) + j, 1), :]),
                                                mv[q][:, j, 0:1], rs[q][:, j:j + 1], ALU.subtract, ALU.mult
                                                ).then_inc(s_C, 1)
                if s.on(0, NB):
                    for j in range(JT):
                        nc.vector.bn_stats(st[:, j, :], flat(XR[:, bass.ds(JT * s.n() + j, 1), :])).then_inc(s_A, 1)
                if s.on(-1, NB):
                    if s.on(0, NB):
                        wait(dve, (s_A, KA * s.n() + JT))
                    wait(dve, (s_hi, s.n()))
                    w = bass.ds(WCH * s.n(-1), WCH)
                    tt(Wl[:, w], Wf[:, w], Wh[:, w].bitcast(F32), ALU.subtract).then_inc(s_lo, 1)
                elif s.on(0, NB):
                    wait(dve, (s_A, KA * s.n() + JT))
                if s.on(0, NB):
                    for j in range(JT):
                        nc.vector.bn_aggr(mv[s.slot()][:, j, :], st[:, j, :]).then_inc(s_A, 1)
                if s.on(-2, NB):
                    wait(dve, (s_sg, s.n(-1)), (s_dn, s.n(-3)))
                    tt(h[s.slot(-2, 2)][:], psU[:], sg[s.slot(-2, 2)][:], ALU.mult).then_inc(s_h, 1)
                if route:
                    m1 = v[:, 3, :]
                    wait(dve, (s_ex, s.pairs(-3)))
                    ch(nc.vector.reduce_sum(v[:, 1, :], ez[:], AX))
                    ch(nc.vector.reciprocal(v[:, 2, :], v[:, 1, :]))
                    ch(tt(pr[:], ez[:], bc(v[:, 2, :]), ALU.mult))

                    def pick(m, out):
                        ch(nc.vector.reduce_max(m, pr[:], AX))
                        ch(tt(eq[:], pr[:], bc(m), ALU.is_equal))
                        ch(tt(eq[:], eq[:], w8b, ALU.mult))
                        ch(nc.vector.reduce_max(v[:, 5, :], eq[:], AX))
                        ch(tt(out, eq[:], bc(v[:, 5, :]), ALU.is_equal))

                    pick(m1, s1[:])
                    ch(nc.vector.scalar_tensor_tensor(out=pr[:], in0=s1[:], scalar=-2.0, in1=pr[:],
                                                      op0=ALU.mult, op1=ALU.add))
                    pick(v[:, 4, :], s2[:])
                    ch(tt(M[s.pair(-3)][:], s1[:], s2[:], ALU.add), hold=False)
                    ch(tt(DD[:, bass.ds(JT * s.n(-3), JP)], v[:, 4, :], m1, ALU.subtract), hold=False)
                    assert ch.k == KD
                if s.on(-3, NB):
                    x = XR[:, bass.ds(JT * s.n(-3), JT), :]
                    wait(dve, (s_dn, s.n(-2)))
                    nc.vector.scalar_tensor_tensor(out=x, in0=psY[:], scalar=0.5, in1=x,
                                                   op0=ALU.mult, op1=ALU.add).then_inc(s_add, 1)
                if route:
                    ce = Chain(dve, s_E, KE * (s.pairs(-3) - 1))
                    rk = psR[:, 0:(JP + 1) * E].rearrange("p (j e) -> p j e", e=E)
                    wait(dve, (s_rk, s.pairs(-3)))
                    ce(tt(po[:], rk[:, 0:JP, :], run[:].unsqueeze(1).broadcast_to([P, JP, E]), ALU.add))
                    ce(tt(run[:], run[:], rk[:, JP, :], ALU.add))
                    for k, pk in enumerate((s1, s2)):
                        ce(tt(eq[:], po[:], pk[:], ALU.mult))
                        ce(nc.vector.reduce_sum(v[:, 6 + k, :], eq[:], AX))
                        ce(nc.vector.tensor_copy(idx[s.pair(-3)][:, k, :], v[:, 6 + k, :]), hold=False)
                    assert ce.k == KE
            run_steps(dve, 0, NB + 3, 8, NB, emit)

        @block.scalar
        def _(act):
            act.wait_ge(s_wf, 32)

            def emit(s):
                if s.r % 2 == 1 and s.on(-3, NB):
                    wait(act, (s_D, KD * (s.pairs(-3) - 1) + 2))
                    nc.scalar.activation(ez[:], z[:], ACT.Exp).then_inc(s_ex, 1)
                if s.on(-1, NB):
                    q = s.slot(-1, 2)
                    wait(act, (s_tp, s.n()), (s_gu, s.n(-2)))
                    nc.scalar.activation(nT[q][:], psT[:], ACT.Identity, bias=bet[:], scale=gam[:]).then_inc(s_nT, 1)
                    q4 = s.slot(-1)
                    wait(act, (s_C, KC * s.n()))
                    nc.scalar.activation(n0[1][q4][:, :, 0:D], n0[0][q4][:, :, 0:D], ACT.Copy).then_inc(s_nb, 1)
                if s.on(-1, NB):
                    wait(act, (s_gu, s.n()), (s_h, s.n(-2)))
                    nc.scalar.activation(sg[q][:], psG[:], ACT.Silu).then_inc(s_sg, 1)
                if s.on(0, NB):
                    w = bass.ds(WCH * s.n(), WCH)
                    nc.scalar.activation(Wh[:, w], Wf[:, w], ACT.Copy).then_inc(s_hi, 1)
            run_steps(act, 0, NB + 2, 4, NB, emit)

        @block.tensor
        def _(pe):
            pe.wait_ge(s_w, 16 * NW)
            pe.wait_ge(s_bf, 2)

            def emit(s):
                if s.on(-1, NB):
                    q4, q = s.slot(-1), s.slot(-1, 2)
                    wait(pe, (s_C, KC * s.n()), (s_nT, s.n(-1)))
                    for j in range(JT):
                        t = nc.tensor.transpose(psT[:, j * P:(j + 1) * P], n0[0][q4][:, j, 0:D], ident[:])
                    t.then_inc(s_tp, 1)
                    wait(pe, (s_nT, s.n()), (s_D, KD * (s.pairs(-1) - 2)))
                    for j in range(JT):
                        at = (q * JT + j) * E
                        t = nc.tensor.matmul(psL[s.pair(-1)][:, at:at + E], nT[q][:, j * P:(j + 1) * P], rT[:],
                                             start=True, stop=True)
                    t.then_inc(s_lg, 1)
                    wait(pe, (s_sg, s.n(-1)), (s_h, s.n(-1)))
                    nc.tensor.matmul(psG[:], sgT[:], nT[q][:], start=True, stop=True)
                    nc.tensor.matmul(psU[:], suT[:], nT[q][:], start=True, stop=True).then_inc(s_gu, 1)
                if s.on(-2, NB):
                    q = s.slot(-2, 2)
                    wait(pe, (s_h, s.n(-1)), (s_add, s.n(-2)))
                    for j in range(JT):
                        t = nc.tensor.matmul(psY[:, j, :], h[q][:, j * P:(j + 1) * P], sdT[:], start=True, stop=True)
                    t.then_inc(s_dn, 1)
                if s.r % 2 == 1 and s.on(-3, NB):
                    m = M[s.pair(-3)]
                    wait(pe, (s_D, KD * s.pairs(-3)), (s_E, KE * (s.pairs(-3) - 1)))
                    nc.tensor.matmul(psR[:, 0:JP * E], trib[:], flat(m[:]), start=True, stop=False,
                                     skip_group_check=True)
                    for j in range(JP):
                        r = nc.tensor.matmul(psR[:, (j + 1) * E:(JP + 1) * E], onesb[:],
                                             m[:, j:j + 1, :].broadcast_to([P, JP - j, E]), start=False,
                                             stop=j == JP - 1, skip_group_check=True)
                    r.then_inc(s_rk, 1)
                if add_attention and s.on(1, NB):
                    oproj(s, 1)

            def oproj(s, off):
                q = s.slot(off)
                wait(pe, (s_os[q], 16 * (s.lap(off) + 1)), (s_oa, s.n(off)))
                nc.tensor.matmul(psE[:], ones[0:1, :], bo[:].unsqueeze(1).broadcast_to([1, JT, D]), start=True,
                                 stop=False, skip_group_check=True)
                for j in range(JT):
                    t = nc.tensor.matmul(psE[:, j, :], Os[q][:, j * P:(j + 1) * P], wo[:], start=False,
                                         stop=j == JT - 1, skip_group_check=True)
                t.then_inc(s_o, 1)

            if add_attention:
                oproj(Step(0, 0), 0)
            run_steps(pe, 0, NB + 2, 8, NB - 4 * add_attention, emit)


def tile_map(K, tag, R):
    nc, T, sb, xd = (K[k] for k in ("nc", "T", "sb", "xd"))
    DD, G1, G2, run, tab = (R[k] for k in ("DD", "G1", "G2", "run", "tab"))
    tag = tag + "m"
    with ExitStack() as c:
        erow = sb(c, tag + "_erow", [P, E])
        part = sb(c, tag + "_part", [P, 1])
        lower = sb(c, tag + "_lower", [P, E, E])
        tau = sb(c, tag + "_tau", [1, ET])
        a = sb(c, tag + "_a", [P, 8, E])
        ti = sb(c, tag + "_ti", [P, 2, E], I32)
        pad = sb(c, tag + "_pad", [P, TR // P, E], U32)
        spare = sb(c, tag + "_spare", [P, SPARE, DX])
        sto = sb(c, tag + "_spareto", [P, SPARE], U32)
        e2 = sb(c, tag + "_e2", [P, NT])
        sh = sb(c, tag + "_sh", [P, NT])
        m = sb(c, tag + "_m", [P, E, E])
        cm = sb(c, tag + "_cm", [1, ET, E])
        tv = sb(c, tag + "_tv", [1, 6, ET])
        S = Sems(nc, c, tag)
        s_w, s_v, s_p, s_a, s_sp, s_x = (S(x) for x in ("w", "chain", "pad", "exp", "spare", "spareout"))
        block = c.enter_context(nc.Block())

        @block.sync
        def _(sp):
            for dst, src in ((erow, "erow"), (part, "part"), (lower, "lower"), (tau, "tau"), (sto, "spareto")):
                sp.dma_start(dst[:], T[src]).then_inc(s_w, 16)
            sp.wait_ge(s_sp, 2)
            sp.dma_start(xd[E * REG:, :].rearrange("(c p) d -> p c d", p=P), spare[:, NPAD:, :]).then_inc(s_x, 16)
            sp.wait_ge(s_x, 16)

        @block.scalar
        def _(act):
            nc.scalar.activation(e2[:], DD[:], ACT.Exp).then_inc(s_a, 1)

        @block.gpsimd
        def _(pool):
            nc.gpsimd.memset(spare[:], 0.0).then_inc(s_sp, 1)
            pool.wait_ge(s_sp, 2)
            pool.wait_ge(s_v, 2 * (TR // P))
            for g in range(TR // P):
                for e in range(E):
                    pool.indirect_dma_start(xd, bass.IndirectOffsetOnAxis(pad[:, g, e:e + 1], 0), spare[:, g * E + e, :],
                                            None                                            ).then_inc(s_p, 16)
            pool.wait_ge(s_p, 16 * E * (TR // P))

        @block.vector
        def _(dve):
            ch = Chain(dve, s_v, 0)
            tt, ts = nc.vector.tensor_tensor, nc.vector.tensor_scalar
            cnt, tf, incl = (a[:, k, :] for k in range(3))
            dve.wait_ge(s_w, 80)
            dve.wait_ge(s_sp, 1)
            nc.vector.tensor_copy(spare[:, :, D].bitcast(U32), sto[:]).then_inc(s_sp, 1)
            for g in range(TR // P):
                ch(ts(a[:, 5, :], run[:], part[:], float(g * P), ALU.add, ALU.add))
                ch(nc.vector.tensor_copy(pad[:, g, :], a[:, 5, :]))
            ch(tt(cnt, run[:], erow[:], ALU.subtract))
            ch(ts(ti[:, 0, :], cnt, float(TR - 1), None, ALU.add))
            ch(ts(ti[:, 1, :], ti[:, 0, :], TR.bit_length() - 1, None, ALU.logical_shift_right))
            ch(nc.vector.tensor_copy(tf, ti[:, 1, :]))
            ch(tt(m[:], lower[:], tf.unsqueeze(1).broadcast_to([P, E, E]), ALU.mult))
            ch(nc.vector.reduce_sum(incl, m[:], AX))
            dve.wait_ge(s_a, 1)
            ch(ts(sh[:], e2[:], 1.0, None, ALU.add))
            ch(nc.vector.reciprocal(G2[:], sh[:]))
            ch(ts(G1[:], G2[:], 0.5, None, ALU.mult))
            ch(tt(G2[:], G1[:], e2[:], ALU.mult))
            ex, nb, ok, t0, t1, t2 = (tv[:, k, :] for k in range(6))
            ch(tt(cm[:], tau[:].unsqueeze(2).broadcast_to([1, ET, E]),
                  incl[0:1, :].unsqueeze(1).broadcast_to([1, ET, E]), ALU.is_ge))
            ch(nc.vector.reduce_sum(ex, cm[:], AX))
            ch(tt(cm[:], cm[:], tf[0:1, :].unsqueeze(1).broadcast_to([1, ET, E]), ALU.mult))
            ch(nc.vector.reduce_sum(nb, cm[:], AX))
            ch(ts(ok, ex, float(E), None, ALU.is_lt))
            ch(tt(t0, ex, ok, ALU.mult))
            ch(nc.vector.tensor_copy(tab[:, 0, :], t0))
            ch(ts(t1, ex, float(REG // TR), None, ALU.mult))
            ch(tt(t2, tau[:], nb, ALU.subtract))
            ch(tt(t1, t1, t2, ALU.add))
            ch(ts(t0, tau[:], float(E * REG // TR - (TOPK * TOK) // TR), None, ALU.add))
            ch(tt(t1, t1, t0, ALU.subtract))
            ch(tt(t1, t1, ok, ALU.mult))
            ch(tt(t2, t1, t0, ALU.add))
            ch(nc.vector.tensor_copy(tab[:, 1, :], t2))


def experts(K, tag, R):
    nc, sb, ps, ident, gam, bet, xd, yd = (K[k] for k in ("nc", "sb", "ps", "ident", "gam", "bet", "xd", "yd"))
    tab, Wh, Wl, Wd = (R[k] for k in ("tab", "Wh", "Wl", "Wd"))
    tag = tag + "x"
    NS = TR // P
    with ExitStack() as c:
        Xs = [sb(c, f"{tag}_Xs{q}", [P, NS, DX]) for q in range(4)]
        to = [sb(c, f"{tag}_to{q}", [P, NS], U32) for q in range(4)]
        none = sb(c, tag + "_none", [P, NS], U32)
        Xf = [sb(c, f"{tag}_Xf{q}", [P, TR]) for q in range(2)]
        Xh = [sb(c, f"{tag}_Xh{q}", [P, TR], F32R) for q in range(2)]
        Xl = [sb(c, f"{tag}_Xl{q}", [P, TR], F32R) for q in range(2)]
        Th = [sb(c, f"{tag}_Th{q}", [P, 2 * FF], F32R) for q in range(2)]
        Tl = [sb(c, f"{tag}_Tl{q}", [P, 2 * FF], F32R) for q in range(2)]
        sg = [sb(c, f"{tag}_sg{q}", [P, FC, TR]) for q in range(2)]
        h = [sb(c, f"{tag}_h{q}", [P, FC, TR]) for q in range(2)]
        Ys = [sb(c, f"{tag}_Ys{q}", [P, NS, D]) for q in range(4)]
        psX = ps(c, tag + "_psX", [P, NS, P])
        psGU = [[ps(c, f"{tag}_psGU{q}{k}", [P, 2, TR]) for k in range(FC)] for q in range(2)]
        psY = ps(c, tag + "_psY", [P, NS, D])
        gate_at, up_at = ((0, 0), (0, 1), (1, 0)), ((2, 0), (2, 1), (1, 1))
        S = Sems(nc, c, tag)
        s_ld = [S(f"in{q}") for q in range(4)]
        s_st = [S(f"out{q}") for q in range(4)]
        s_tx, s_xf, s_hl, s_gu, s_sg, s_h, s_dn, s_y, s_wl, s_to, s_no = (
            S(x) for x in ("tx", "xf", "hilo", "gateup", "silu", "hidden", "down", "y", "wlo", "dest", "none"))
        block = c.enter_context(nc.Block())
        LOOP = (4, ET - 4)

        def expert(eng, s, off):
            return eng.value_load(tab[0:1, 0, bass.ds(s.n(off), 1)], min_val=0, max_val=E - 1)

        @block.sync
        def _(sp):
            def load(s, off):
                q = s.slot(off)
                row = sp.value_load(tab[0:1, 1, bass.ds(s.n(off), 1)], min_val=0, max_val=(E * REG + (SPARE - NPAD) * P) // TR - 1)
                wait(sp, (s_tx, s.n(off - 3)), (s_to, s.n(off - 3)))
                sp.dma_start(Xs[q][:], xd[bass.ds(row * TR, TR), :].rearrange("(g p) d -> p g d", p=P)
                             ).then_inc(s_ld[q], 16)

            for k in range(2):
                load(Step(0, k), 0)

            def emit(s):
                if s.on(2, ET):
                    load(s, 2)
            run_steps(sp, 0, ET, *LOOP, emit)

        @block.gpsimd
        def _(pool):
            nc.gpsimd.memset(none[:], 0).then_inc(s_no, 1)
            pool.wait_ge(s_no, 1)

            def emit(s):
                if s.on(-2, ET):
                    wait(pool, (s_to, s.n(-1)), (s_y, s.n(-1)))
                if s.on(0, ET):
                    q = s.slot()
                    wait(pool, (s_ld[q], 16 * (s.lap() + 1)), (s_st[q], 16 * NS * s.lap()))
                    col = Xs[q][:, :, D].bitcast(U32)
                    nc.gpsimd.tensor_tensor(to[q][:], col, none[:], ALU.add).then_inc(s_to, 1)
                if s.on(-2, ET):
                    q = s.slot(-2)
                    for g in range(NS):
                        pool.indirect_dma_start(yd, bass.IndirectOffsetOnAxis(to[q][:, g:g + 1], 0), Ys[q][:, g, :],
                                                None).then_inc(s_st[q], 16)
            run_steps(pool, 0, ET + 2, 4, ET, emit)
            for q in range(4):
                pool.wait_ge(s_st[q], 16 * NS * (ET // 4))

        @block.tensor
        def _(pe):
            def tx(s, off):
                q = s.slot(off)
                wait(pe, (s_ld[q], 16 * (s.lap(off) + 1)), (s_xf, s.n(off)))
                for g in range(NS):
                    m = nc.tensor.transpose(psX[:, g, :], Xs[q][:, g, 0:D], ident[:])
                m.then_inc(s_tx, 1)

            tx(Step(0, 0), 0)

            def emit(s):
                if s.on(1, ET):
                    tx(s, 1)
                if s.on(0, ET):
                    q = s.slot(0, 2)
                    wait(pe, (s_hl, 3 * s.n(1)))
                    for k in range(FC):
                        for at, (bank, half) in ((k * P, gate_at[k]), (FF + k * P, up_at[k])):
                            dst = psGU[q][bank][:, half, :]
                            wh, wl = (w[:, at:at + P] for w in (Th[q], Tl[q]))
                            nc.tensor.matmul(dst, wh, Xh[q][:], start=True, stop=False)
                            nc.tensor.matmul(dst, wh, Xl[q][:], start=False, stop=False)
                            m = nc.tensor.matmul(dst, wl, Xh[q][:], start=False, stop=True)
                    m.then_inc(s_gu, 1)
                if s.on(-1, ET):
                    q = s.slot(-1, 2)
                    e = expert(pe, s, -1)
                    wait(pe, (s_h, 2 * s.n()), (s_y, s.n(-1)))
                    for k in range(FC):
                        w = Wd[:, bass.ds(e * FC + k, 1), :].rearrange("p o n -> p (o n)")
                        for g in range(NS):
                            m = nc.tensor.matmul(psY[:, g, :], h[q][:, k, g * P:(g + 1) * P], w,
                                                 start=k == 0 and g == 0, stop=k == FC - 1 and g == NS - 1,
                                                 skip_group_check=True)
                    m.then_inc(s_dn, 1)
            run_steps(pe, 0, ET + 1, *LOOP, emit)

        @block.scalar
        def _(act):
            def xf(s, off):
                wait(act, (s_tx, s.n(off + 1)), (s_hl, 3 * s.n(off - 1)))
                nc.scalar.activation(Xf[s.slot(off, 2)][:], flat(psX[:]), ACT.Identity, bias=bet[:], scale=gam[:]
                                     ).then_inc(s_xf, 1)

            def weights(s, off):
                e = expert(act, s, off)
                nc.scalar.activation(Tl[s.slot(off, 2)][:], Wl[:, bass.ds(e * (2 * FF), 2 * FF)].bitcast(F32),
                                     ACT.Copy).then_inc(s_wl, 1)

            for k in range(2):
                weights(Step(0, k), 0)
            xf(Step(0, 0), 0)

            def emit(s):
                if s.on(1, ET):
                    xf(s, 1)
                if s.on(0, ET):
                    q = s.slot(0, 2)
                    wait(act, (s_gu, s.n(1)), (s_h, 2 * s.n(-1)))
                    nc.scalar.activation(sg[q][:, 0:2, :], psGU[q][0][:], ACT.Silu).then_inc(s_sg, 1)
                    nc.scalar.activation(sg[q][:, 2, :], psGU[q][1][:, 0, :], ACT.Silu).then_inc(s_sg, 1)
                if s.on(2, ET):
                    weights(s, 2)
            run_steps(act, 0, ET, *LOOP, emit)

        @block.vector
        def _(dve):
            def hilo(s, off):
                q = s.slot(off, 2)
                e = expert(dve, s, off)
                wait(dve, (s_xf, s.n(off + 1)), (s_gu, s.n(off - 1)))
                nc.vector.tensor_copy(Xh[q][:], Xf[q][:]).then_inc(s_hl, 1)
                nc.vector.tensor_copy(Th[q][:], Wh[:, bass.ds(e * (2 * FF), 2 * FF)].bitcast(F32)).then_inc(s_hl, 1)
                wait(dve, (s_hl, 3 * s.n(off) + 1))
                nc.vector.tensor_tensor(Xl[q][:], Xf[q][:], Xh[q][:].bitcast(F32), ALU.subtract).then_inc(s_hl, 1)

            hilo(Step(0, 0), 0)

            def emit(s):
                if s.on(-2, ET):
                    q4 = s.slot(-2)
                    wait(dve, (s_dn, s.n(-1)), (s_st[q4], 16 * NS * s.lap(-2)))
                    nc.vector.tensor_copy(Ys[q4][:], psY[:]).then_inc(s_y, 1)
                if s.on(1, ET):
                    hilo(s, 1)
                if s.on(0, ET):
                    q = s.slot(0, 2)
                    wait(dve, (s_sg, 2 * s.n() + 1), (s_dn, s.n(-1)))
                    nc.vector.tensor_tensor(h[q][:, 0:2, :], psGU[q][2][:], sg[q][:, 0:2, :], ALU.mult
                                            ).then_inc(s_h, 1)
                    wait(dve, (s_sg, 2 * s.n(1)))
                    nc.vector.tensor_tensor(h[q][:, 2, :], psGU[q][1][:, 1, :], sg[q][:, 2, :], ALU.mult
                                            ).then_inc(s_h, 1)
            run_steps(dve, 0, ET + 2, 8, ET - 4, emit)


def combine(K, tag, R, last):
    nc, T, sb, ps, XR, ident, mhalf, eps, yd, rec = (
        K[k] for k in ("nc", "T", "sb", "ps", "XR", "ident", "mhalf", "eps", "yd", "rec"))
    G1, G2 = R["G1"], R["G2"]
    tag = tag + "c"
    with ExitStack() as c:
        Y = [sb(c, f"{tag}_Y{q}", [P, TOPK, JT, D]) for q in range(4)]
        S = Sems(nc, c, tag)
        s_cb = S("combined")
        s_ga = [S(f"loaded{q}") for q in range(4)]
        s_st = [S(f"stored{q}") for q in range(4)]
        KC, KA, KR = 2 * JT, 2 * JT, 5
        if not last:
            s_A, s_rs, s_C, s_tp, s_xT, s_mm, s_f, s_r, s_w, s_bk = (
                S(x) for x in ("stats", "rstd", "normed", "transp", "xT", "qkv", "qkvf", "rec", "w", "scaled"))
            wq, wk, wv = (sb(c, f"{tag}_{w}", [P, D]) for w in ("WqT", "WkT", "WvT"))
            bq, bk, bks, bv = (sb(c, f"{tag}_{w}", [P, 1]) for w in ("bq", "bk", "bks", "bv"))
            st = sb(c, tag + "_stats", [P, JT, 6])
            mv = [sb(c, f"{tag}_mv{q}", [P, JT, 2]) for q in range(4)]
            ve = sb(c, tag + "_ve", [P, JT])
            rs = [sb(c, f"{tag}_rs{q}", [P, JT]) for q in range(4)]
            xn = [sb(c, f"{tag}_xn{q}", [P, JT, D]) for q in range(2)]
            xT = sb(c, tag + "_xT", [P, L])
            Qf, Kf, Vf = ([sb(c, f"{tag}_{w}{q}", [P, L]) for q in range(2)] for w in ("Qf", "Kf", "Vf"))
            rc = [sb(c, f"{tag}_rec{q}", [P, REC], F32R) for q in range(4)]
            psT = ps(c, tag + "_psT", [P, L])
            psQ = [ps(c, f"{tag}_psQ{q}", [P, L]) for q in range(3)]
        isq = float(1.0 / np.sqrt(HD))
        block = c.enter_context(nc.Block())

        @block.sync
        def _(sp):
            if not last:
                for dst, src in ((wq, "WqT"), (wk, "WkT"), (wv, "WvT"), (bq, "bq"), (bk, "bk"), (bv, "bv")):
                    sp.dma_start(dst[:], T[src]).then_inc(s_w, 16)

            yv = yd[0:TOPK * TOK, :].rearrange("(k n p) d -> p k n d", k=TOPK, p=P)

            def load(s, off):
                q = s.slot(off)
                wait(sp, (s_cb, KC * s.n(off - 3)))
                for k in range(TOPK):
                    sp.dma_start(Y[q][:, k, :, :], yv[:, k, bass.ds(JT * s.n(off), JT), :]).then_inc(s_ga[q], 16)

            for k in range(2):
                load(Step(0, k), 0)

            def emit(s):
                if s.on(2, NB):
                    load(s, 2)
                if last and s.on(-1, NB):
                    wait(sp, (s_cb, KC * s.n()))
                    ov = T["out"].rearrange("(n p) d -> p n d", p=P)[:, bass.ds(JT * s.n(-1), JT), :]
                    sp.dma_start(ov, XR[:, bass.ds(JT * s.n(-1), JT), :]).then_inc(s_st[s.slot(-1)], 16)
                if not last and s.on(-3, NB):
                    q, b = s.slot(-3), s.n(-3)
                    wait(sp, (s_r, KR * s.n(-2)))
                    sp.dma_start(rec[bass.ds(b, 1), :, :].rearrange("a p n -> (a p) n"), rc[q][:].bitcast(F32)
                                 ).then_inc(s_st[q], 16)
            run_steps(sp, 0, NB + 3, 4, NB - 4, emit)
            for q in range(4):
                sp.wait_ge(s_st[q], 16 * (NB // 4))

        @block.gpsimd
        def _(pool):
            if last:
                return

            def emit(s):
                if s.on(-1, NB):
                    q = s.slot(-1)
                    wait(pool, (s_A, KA * s.n()))
                    nc.gpsimd.tensor_tensor(ve[:], mv[q][:, :, 1], eps[:], ALU.add).then_inc(s_rs, 1)
                    wait(pool, (s_rs, 2 * s.n(-1) + 1), (s_C, JT * s.n(-3)))
                    nc.gpsimd.tensor_tensor(rs[q][:], ve[:], mhalf[:], ALU.pow).then_inc(s_rs, 1)
            run_steps(pool, 0, NB + 1, 4, NB, emit)

        @block.vector
        def _(dve):
            def emit(s):
                if s.on(-1, NB):
                    q = s.slot(-1)
                    wait(dve, (s_ga[q], 16 * TOPK * (s.lap(-1) + 1)))
                    for k, gate in ((0, G1), (1, G2)):
                        for j in range(JT):
                            t = JT * s.n(-1) + j
                            x = XR[:, bass.ds(t, 1), :].rearrange("p o d -> p (o d)")
                            nc.vector.scalar_tensor_tensor(out=x, in0=Y[q][:, k, j, :], scalar=gate[:, bass.ds(t, 1)],
                                                           in1=x, op0=ALU.mult, op1=ALU.add).then_inc(s_cb, 1)
                        wait(dve, (s_cb, KC * s.n(-1) + JT * (k + 1)))
                if last:
                    return
                if s.on(-1, NB):
                    wait(dve, (s_A, KA * s.n(-1)))
                if s.on(-2, NB):
                    q = s.slot(-2)
                    wait(dve, (s_rs, 2 * s.n(-1)), (s_tp, s.n(-3)))
                    for j in range(JT):
                        nc.vector.tensor_scalar(xn[s.slot(-2, 2)][:, j, :],
                                                flat(XR[:, bass.ds(JT * s.n(-2) + j, 1), :]),
                                                mv[q][:, j, 0:1], rs[q][:, j:j + 1], ALU.subtract, ALU.mult
                                                ).then_inc(s_C, 1)
                if s.on(-1, NB):
                    for j in range(JT):
                        nc.vector.bn_stats(st[:, j, :], flat(XR[:, bass.ds(JT * s.n(-1) + j, 1), :])).then_inc(s_A, 1)
                    wait(dve, (s_A, KA * s.n(-1) + JT))
                if s.on(-3, NB):
                    q, q2 = s.slot(-3), s.slot(-3, 2)
                    r = rc[q]
                    base = KR * s.n(-3)
                    wait(dve, (s_f, 3 * s.n(-2)), (s_st[q], 16 * s.lap(-3)))
                    nc.vector.tensor_copy(r[:, 2 * L:3 * L], Qf[q2][:]).then_inc(s_r, 1)
                    nc.vector.tensor_copy(r[:, 0:L], Kf[q2][:]).then_inc(s_r, 1)
                    wait(dve, (s_r, base + 2))
                    nc.vector.tensor_tensor(r[:, 3 * L:4 * L], Qf[q2][:], r[:, 2 * L:3 * L].bitcast(F32), ALU.subtract
                                            ).then_inc(s_r, 1)
                    nc.vector.tensor_tensor(r[:, L:2 * L], Kf[q2][:], r[:, 0:L].bitcast(F32), ALU.subtract
                                            ).then_inc(s_r, 1)
                    nc.vector.transpose(r[:, 4 * L:5 * L].bitcast(F32), Vf[q2][:]).then_inc(s_r, 1)
                if s.on(-1, NB):
                    for j in range(JT):
                        nc.vector.bn_aggr(mv[s.slot(-1)][:, j, :], st[:, j, :]).then_inc(s_A, 1)
            run_steps(dve, 0, NB + 3, 8, NB, emit)

        if last:
            return

        @block.scalar
        def _(act):
            act.wait_ge(s_w, 96)
            nc.scalar.activation(bks[:], bk[:], ACT.Copy, scale=isq).then_inc(s_bk, 1)
            act.wait_ge(s_bk, 1)

            def emit(s):
                if s.on(-2, NB):
                    q2 = s.slot(-2, 2)
                    wait(act, (s_tp, s.n(-1)), (s_mm, 3 * s.n(-2)))
                    nc.scalar.activation(xT[:], psT[:], ACT.Copy).then_inc(s_xT, 1)
                    wait(act, (s_r, KR * s.n(-3)))
                    for n, (dst, bias, scale) in enumerate(((Qf, bq, 1.0), (Kf, bks, isq), (Vf, bv, 1.0))):
                        wait(act, (s_mm, 3 * s.n(-2) + n + 1))
                        nc.scalar.activation(dst[q2][:], psQ[n][:], ACT.Identity, bias=bias[:], scale=scale
                                             ).then_inc(s_f, 1)
            run_steps(act, 0, NB + 2, 4, NB, emit)

        @block.tensor
        def _(pe):
            pe.wait_ge(s_w, 96)

            def emit(s):
                if s.on(-2, NB):
                    wait(pe, (s_C, JT * s.n(-1)), (s_xT, s.n(-2)))
                    for j in range(JT):
                        m = nc.tensor.transpose(psT[:, j * P:(j + 1) * P], xn[s.slot(-2, 2)][:, j, :], ident[:])
                    m.then_inc(s_tp, 1)
                    wait(pe, (s_xT, s.n(-1)), (s_f, 3 * s.n(-2)))
                    for n, w in enumerate((wq, wk, wv)):
                        nc.tensor.matmul(psQ[n][:], w[:], xT[:], start=True, stop=True).then_inc(s_mm, 1)
            run_steps(pe, 0, NB + 2, 4, NB, emit)


def attention(K):
    nc, T, sb, ps, rec, rsd, otd = (K[k] for k in ("nc", "T", "sb", "ps", "rec", "rsd", "otd"))
    with ExitStack() as c:
        RA = sb(c, "rel_hi", [P, RELW], F32R)
        RB = sb(c, "rel_lo", [P, RELW], F32R)
        RF = sb(c, "rel_f32", [P, RELW])
        maskh = sb(c, "mask_head", [P, H])
        maska = sb(c, "mask_a", [P, A8])
        KQ = sb(c, "record_ring", [P, 2, REC], F32R)
        M0 = sb(c, "q_by_query_ring", [P, 2, H, NQ])
        NS = 8
        SQ = [sb(c, f"stat_q{s}", [P, 2, H, A8], F32R) for s in range(NS)]
        SR = [sb(c, f"stat_r{s}", [P, H, A8], F32R) for s in range(NS)]
        nmx = sb(c, "neg_max", [P, 4])
        Pr = [sb(c, f"probs{s}", [P, L]) for s in range(4)]
        PT = [sb(c, f"probs_T{s}", [P, KEYS32, 4, GT, A8]) for s in range(2)]
        W = sb(c, "values_diag", [P, 4, KEYS32, 4, HD])
        rs = sb(c, "row_sum", [P, 2, GT])
        rb = sb(c, "row_sum_T", [P, 2, A8, GT])
        ri = sb(c, "recip_sum", [P, A8, GT])
        OT = sb(c, "attn_out", [P, A8, NQ])
        psS = [ps(c, f"ps_scores{s}", [P, L]) for s in range(4)]
        psO = [ps(c, f"ps_out{s}", [P, GT, A8]) for s in range(2)]
        S = Sems(nc, c, "att")
        (s_rf, s_rh, s_rec, s_m0, s_ex, s_sc, s_mx, s_p, s_tr, s_wz, s_we, s_pv, s_rs, s_rb, s_ri, s_o, s_ot, s_mk) = (
            S(x) for x in ("relf", "rel", "rec", "m0", "expanded", "scores", "max", "probs", "transposed", "wzero",
                           "wexp", "pv", "rsum_out", "rsum_in", "recip", "out", "out_st", "masks"))
        block = c.enter_context(nc.Block())

        @block.sync
        def _(sp):
            for part in range(2):
                for a in range(A8):
                    p0 = part * 64 + a * HD
                    off = L - 1 - (NQ - 1) - NQ * a
                    sp.dma_start(RF[p0:p0 + HD, :], T["relT"][:, off:off + RELW]).then_inc(s_rf, 16)
            sp.dma_start(maskh[:], T["maskh"]).then_inc(s_mk, 16)
            sp.dma_start(maska[:], T["maska"]).then_inc(s_mk, 16)

            def load(b, par):
                sp.dma_start(KQ[:, bass.ds(par, 1), :].rearrange("p o n -> p (o n)").bitcast(F32),
                             rec[bass.ds(b, 1), :, :].rearrange("a p n -> (a p) n")).then_inc(s_rec, 16)
                for part in range(2):
                    for a in range(A8):
                        p0 = part * 64 + a * HD
                        at = (2 + part) * L + a * NQ
                        src = rec[bass.ds(b, 1), :, at:at + NQ].rearrange("b (h d) t -> d (b h) t", d=HD)
                        sp.dma_start(M0[p0:p0 + HD, bass.ds(par, 1), :, :].rearrange("p o h t -> p (o h) t"), src
                                     ).then_inc(s_m0, 16)

            def seq(b, first, last):
                wait(sp, (s_rec, 16 * (b + 1)), (s_m0, 256 * (b + 1)))
                for g in range(NG):
                    G = b * NG + g
                    wait(sp, (s_p, (G + 1) * GT))
                    sp.dma_start(rsd[bass.ds(G, 1), :, :].rearrange("o p t -> (o p) t"), rs[:, g % 2, :]
                                 ).then_inc(s_rs, 16)
                    wait(sp, (s_rs, 16 * (G + 1)), (s_ri, G - 1), (s_rb, 64 * G))
                    for hh in range(4):
                        src = rsd[bass.ds(G, 1), :, :].rearrange("o (k hh a) t -> hh (o k) (a t)", k=4, hh=4)[hh]
                        src = src.unsqueeze(1).broadcast_to([4, HD, A8 * GT])
                        dst = rb[32 * hh:32 * hh + 32, g % 2, :, :].rearrange("p a t -> p (a t)")
                        sp.dma_start(dst, src).then_inc(s_rb, 16)
                    if g == 0 and not first:
                        wait(sp, (s_o, b * NG))
                        sp.dma_start(otd[bass.ds(b - 1, 1), :, :].rearrange("a p n -> (a p) n"),
                                     OT[:].rearrange("p a t -> p (a t)")).then_inc(s_ot, 16)
                    if g == 1 and not last:
                        wait(sp, (s_sc, b * NQ), (s_we, 4 * b))
                        load(b + 1, (b + 1) % 2)

            load(0, 0)
            seq(0, True, False)
            with sp.Fori(1, B - 1) as b:
                seq(b, False, False)
            seq(B - 1, False, True)
            sp.wait_ge(s_o, B * NG)
            sp.dma_start(otd[B - 1], OT[:].rearrange("p a t -> p (a t)")).then_inc(s_ot, 16)
            sp.wait_ge(s_ot, 16 * B)

        @block.gpsimd
        def _(pool):
            pool.wait_ge(s_mk, 32)
            mh = maskh[:].unsqueeze(2).broadcast_to([P, H, A8]).unsqueeze(1).broadcast_to([P, 2, H, A8])
            ma = maska[:].unsqueeze(1).broadcast_to([P, H, A8])

            def seq(b, first):
                pool.wait_ge(s_rec, 16 * (b + 1))
                pool.wait_ge(s_m0, 256 * (b + 1))
                par = b % 2
                for t in range(NQ):
                    n = b * NQ + t
                    s = t % NS
                    if not (first and t < NS):
                        pool.wait_ge(s_sc, n - NS + 1)
                    q = KQ[:, bass.ds(par, 1), 2 * L:4 * L].bitcast(F32).rearrange(
                        "p o (c a t) -> p (o c) a t", c=2, a=A8)[:, :, :, t]
                    q = q.unsqueeze(2).broadcast_to([P, 2, H, A8])
                    nc.gpsimd.tensor_tensor(SQ[s][:], q, mh, ALU.mult).then_inc(s_ex, 1)
                    m0 = M0[:, bass.ds(par, 1), :, t].rearrange("p o h -> p (o h)")
                    nc.gpsimd.tensor_tensor(SR[s][:], m0.unsqueeze(2).broadcast_to([P, H, A8]), ma, ALU.mult
                                            ).then_inc(s_ex, 1)

            seq(0, True)
            with pool.Fori(1, B) as b:
                seq(b, False)

        @block.tensor
        def _(pe):
            pe.wait_ge(s_rh, 2)

            def values(G, par, first2, lo=0, hi=4 * KEYS32):
                if lo == 0:
                    pe.wait_ge(s_tr, (G + 1) * GT)
                    if not first2:
                        pe.wait_ge(s_o, G - 1)
                for n in range(lo, min(hi, 4 * KEYS32)):
                    r, hh = n // 4, n % 4
                    m = nc.tensor.matmul(psO[par][32 * hh:32 * hh + 32, :, :].rearrange("p t a -> p (t a)"),
                                         W[:, hh, r, :, :].rearrange("p k d -> p (k d)"),
                                         PT[par][:, r, hh, :, :].rearrange("p t a -> p (t a)"),
                                         start=(r == 0), stop=(r == KEYS32 - 1))
                if hi >= 4 * KEYS32:
                    m.then_inc(s_pv, 1)

            def seq(b, first):
                pe.wait_ge(s_rec, 16 * (b + 1))
                par = b % 2
                for t in range(NQ):
                    n = b * NQ + t
                    s, bank = t % NS, t % 4
                    pe.wait_ge(s_ex, 2 * (n + 1))
                    if not (first and t < 4):
                        pe.wait_ge(s_p, n - 3)
                    khi = KQ[:, bass.ds(par, 1), 0:L].rearrange("p o n -> p (o n)")
                    klo = KQ[:, bass.ds(par, 1), L:2 * L].rearrange("p o n -> p (o n)")
                    qh = SQ[s][:, 0, :, :].rearrange("p h a -> p (h a)")
                    ql = SQ[s][:, 1, :, :].rearrange("p h a -> p (h a)")
                    qr = SR[s][:].rearrange("p h a -> p (h a)")
                    w0 = NQ - 1 - t
                    nc.tensor.matmul(psS[bank][:], qr, RA[:, w0:w0 + L], start=True, stop=False)
                    nc.tensor.matmul(psS[bank][:], qr, RB[:, w0:w0 + L], start=False, stop=False)
                    nc.tensor.matmul(psS[bank][:], qh, khi, start=False, stop=False)
                    nc.tensor.matmul(psS[bank][:], qh, klo, start=False, stop=False)
                    nc.tensor.matmul(psS[bank][:], ql, khi, start=False, stop=True).then_inc(s_sc, 1)
                    g, k = t // GT, t % GT - VT0
                    each = VEACH if g else 2 * KEYS32 // 4
                    if k >= 0 and k * each < 4 * KEYS32 and not (first and g == 0):
                        if g == 1 and k == 0:
                            pe.wait_ge(s_we, 4 * (b + 1))
                        values(b * NG + g - 1, (g - 1) % 2, first and g < 3, k * each, (k + 1) * each)

            seq(0, True)
            with pe.Fori(1, B) as b:
                seq(b, False)
            values(B * NG - 1, 1, False)

        @block.vector
        def _(dve):
            nc.vector.memset(W[:], 0.0).then_inc(s_wz, 1)
            dve.wait_ge(s_rf, 256)
            nc.vector.tensor_copy(RA[:], RF[:]).then_inc(s_rh, 1)
            dve.wait_ge(s_rh, 1)
            nc.vector.tensor_tensor(RB[:], RF[:], RA[:].bitcast(F32), ALU.subtract).then_inc(s_rh, 1)

            def transpose(b, t, first):
                dve.wait_ge(s_p, b * NQ + t + 1)
                g, tt = t // GT, t % GT
                if tt == 0 and not (first and g < 2):
                    dve.wait_ge(s_pv, b * NG + g - 1)
                nc.vector.transpose(PT[g % 2][:, :, :, tt, :],
                                    Pr[t % 4][:].rearrange("p (r x) -> p r x", x=32)).then_inc(s_tr, 1)

            def norm(G, g, first2, b):
                dve.wait_ge(s_rb, 64 * (G + 1))
                if not (first2 and g == 0):
                    dve.wait_ge(s_o, G)
                nc.vector.reciprocal(ri[:], rb[:, g % 2, :, :]).then_inc(s_ri, 1)
                dve.wait_ge(s_ri, G + 1)
                dve.wait_ge(s_pv, G + 1)
                if g == 0 and not first2:
                    dve.wait_ge(s_ot, 16 * b)
                nc.vector.tensor_tensor(OT[:, :, g * GT:(g + 1) * GT].rearrange("p a t -> p t a"), psO[g % 2][:],
                                        ri[:].rearrange("p a t -> p t a"), ALU.mult).then_inc(s_o, 1)

            def seq(b, first):
                for t in range(NQ):
                    n = b * NQ + t
                    dve.wait_ge(s_sc, n + 1)
                    if not (first and t < 4):
                        dve.wait_ge(s_p, n - 3)
                    nc.vector.reduce_max(nmx[:, t % 4:t % 4 + 1], psS[t % 4][:], AX, negate=True).then_inc(s_mx, 1)
                    if t >= 1:
                        transpose(b, t - 1, first)
                    elif not first:
                        transpose(b - 1, NQ - 1, False)
                    if t % GT == 2:
                        g = t // GT
                        if g >= 2:
                            norm(b * NG + g - 2, g - 2, first, b)
                        elif not first:
                            norm(b * NG + g - 2, NG + g - 2, False, b - 1)

            seq(0, True)
            with dve.Fori(1, B) as b:
                seq(b, False)
            transpose(B - 1, NQ - 1, False)
            norm(B * NG - 2, NG - 2, False, B - 1)
            norm(B * NG - 1, NG - 1, False, B - 1)

        @block.scalar
        def _(act):
            def seq(b, first):
                for t in range(NQ):
                    n = b * NQ + t
                    g, tt = t // GT, t % GT
                    act.wait_ge(s_mx, n + 1)
                    if not (first and t < 4):
                        act.wait_ge(s_tr, n - 3)
                    if tt == 0 and not (first and g < 2):
                        act.wait_ge(s_rs, 16 * (b * NG + g - 1))
                    nc.scalar.activation(Pr[t % 4][:], psS[t % 4][:], ACT.Exp, bias=nmx[:, t % 4:t % 4 + 1],
                                         accum_out=rs[:, g % 2, tt:tt + 1]).then_inc(s_p, 1)
                    if 11 <= t < 15:
                        k = t - 11
                        if first:
                            act.wait_ge(s_wz, 1)
                        else:
                            act.wait_ge(s_pv, b * NG)
                        act.wait_ge(s_rec, 16 * (b + 1))
                        p = slice(32 * k, 32 * k + 32)
                        src = KQ[p, bass.ds(b % 2, 1), 4 * L:5 * L].bitcast(F32).rearrange(
                            "p o (r hh d) -> p (o hh) r d", hh=4, d=HD)
                        nc.scalar.activation(W[p, :, :, k, :], src, ACT.Copy).then_inc(s_we, 1)

            seq(0, True)
            with act.Fori(1, B) as b:
                seq(b, False)

_F = np.float32


def kernel(**inputs):
    import concourse.bacc as _bacc
    from concourse.bass_utils import run_bass_kernel_spmd as _run

    a = {k[3:]: np.asarray(v) for k, v in inputs.items()}
    gu, dn = a["ffn_gate_up_w"], a["ffn_down_w"]
    sgu, sdn = a["ffn_shared_gate_up_w"], a["ffn_shared_down_w"]

    rel = a["attn_rel_emb"]
    rel = np.concatenate([rel[MAXLEN - 1:], rel, np.repeat(rel[-1:], L - 1 - (MAXLEN - 1), axis=0)])
    arrays = {
        "x": a["attn_x"].reshape(TOK, D),
        "ident": np.eye(P, dtype=_F),
        "w8": np.broadcast_to(np.arange(E, 0, -1, dtype=_F), (P, E)),
        "maskh": np.kron(np.eye(H, dtype=_F), np.ones((HD, 1), _F)),
        "maska": np.concatenate([np.kron(np.eye(A8, dtype=_F), np.ones((HD, 1), _F))] * 2),
        "gamma": a["ffn_ln_gamma"].reshape(D, 1),
        "beta": a["ffn_ln_beta"].reshape(D, 1),
        "routerT": a["ffn_router_w"].T,
        "erow": np.broadcast_to(np.arange(E, dtype=_F) * _F(REG), (P, E)),
        "tri": np.triu(np.ones((P, P), _F), 1),
        "ones": np.ones((P, P), _F),
        "part": np.arange(P, dtype=_F).reshape(P, 1),
        "tid": np.arange(TOPK * TOK, dtype=np.uint32).reshape(TOPK, NT, P).transpose(2, 0, 1),
        "spareto": (TOPK * TOK + np.arange(SPARE * P, dtype=np.uint32)).reshape(SPARE, P).T,
        "lower": np.broadcast_to(np.tril(np.ones((E, E), _F)), (P, E, E)),
        "tau": np.arange(ET, dtype=_F).reshape(1, ET),
        "shG": sgu[:SFF].T, "shU": sgu[SFF:].T, "shD": sdn.T,
        "WguT": gu.reshape(E * 2 * FF, D).T,
        "WdT": dn.transpose(0, 2, 1).reshape(E * FC, P, D).transpose(1, 0, 2),
        "WqT": a["attn_Wq"].T, "WkT": a["attn_Wk"].T, "WvT": a["attn_Wv"].T,
        "bq": a["attn_bq"].reshape(D, 1), "bk": a["attn_bk"].reshape(D, 1), "bv": a["attn_bv"].reshape(D, 1),
        "WoT": a["attn_Wo"].T.reshape(4, 4, HD, D).transpose(1, 0, 2, 3).reshape(D, D),
        "bo": a["attn_bo"].reshape(1, D),
        "relT": rel.T,
    }
    arrays = {f"in_{k}": np.ascontiguousarray(v) for k, v in arrays.items()}
    nc = _bacc.Bacc("TRN2", target_bir_lowering=False, num_devices=1)
    T = {k[3:]: nc.dram_tensor(k, v.shape, U32 if v.dtype == np.uint32 else F32, kind="ExternalInput").ap()
         for k, v in arrays.items()}
    T["out"] = nc.dram_tensor("out", (TOK, D), F32, kind="ExternalOutput").ap()
    build(nc, T)
    r = _run(nc, [arrays], core_ids=[0])
    return r.results[0]["out"].reshape(B, L, D)
```
